# Optimizing a Trainium2 kernel written in Bass

```python
import numpy as np
import jax
import jax.numpy as jnp

def _softmax(x, axis=-1):
    return jax.nn.softmax(x, axis=axis)

def _gelu(x):
    return jax.nn.gelu(x, approximate=True)

def _silu(x):
    return jax.nn.silu(x)

def _sigmoid(x):
    return jax.nn.sigmoid(x)

def _layernorm(x, axis=-1, eps=1e-05):
    m = jnp.mean(x, axis=axis, keepdims=True)
    v = jnp.var(x, axis=axis, keepdims=True)
    return (x - m) / jnp.sqrt(v + eps)

def _scatter_add(tgt, idx, src, axis=0):
    return tgt.at[idx].add(src)

def _segment_sum(src, seg, n):
    return jax.ops.segment_sum(src, seg, n)
kernel_name = 'mk_decoder_postln_d1_seqx_r8_23420b'

def setup_inputs(seed: int=0):
    np.random.seed(seed)
    _w = jnp.asarray

    def _rec_inputs():
        import jax
        import jax.numpy as jnp
        _rk = jax.random.key(seed)
        x = -7.109e-05 + 0.9999 * jax.random.normal(jax.random.fold_in(_rk, 1), (8, 128, 512), jnp.float32)
        _lenS = 128 - jax.random.randint(jax.random.fold_in(_rk, 7), (8,), 0, max(1, 128 // 4) + 1, jnp.int32)
        _lenS2 = 128 - jax.random.randint(jax.random.fold_in(_rk, 8), (8,), 0, max(1, 128 // 4) + 1, jnp.int32)
        _ctx_4096P = jax.random.normal(jax.random.fold_in(_rk, 11), (8, 16, 512), jnp.float32)
        _ctx_4096c = jax.random.dirichlet(jax.random.fold_in(_rk, 511), 0.3 * jnp.ones((16,), jnp.float32), (8, 128))
        _ctx_4096t = jnp.einsum('bsk,bkd->bsd', _ctx_4096c, _ctx_4096P)
        _ctx_4096t = _ctx_4096t * jax.lax.rsqrt(jnp.mean(jnp.square(_ctx_4096t)) + 1e-12) * 0.953939
        ctx_4096 = -0.00010331 + 0.999899 * (_ctx_4096t + 0.3 * jax.random.normal(jax.random.fold_in(_rk, 611), (8, 128, 512), jnp.float32))
        return (x, ctx_4096)
    x, ctx_4096 = _rec_inputs()

    def _L0_attn_setup():
        import jax, jax.numpy as jnp
        import numpy as np
        D_MODEL = 512
        D_XB = 128
        D_INNER = 512
        HEADDIM = 128
        DSTATE = 128
        NHEADS = D_INNER // HEADDIM
        DCONV = 4
        INTER = 1792
        EPS = 1e-05
        CHUNK = 128

        def rmsnorm(x, w):
            return x * jax.lax.rsqrt(jnp.mean(x * x, axis=-1, keepdims=True) + EPS) * w

        def silu(x):
            return x * jax.nn.sigmoid(x)

        def mamba2(x, w_in, conv_w, conv_b, A_log, D, dt_bias, w_out):
            B, L, _ = x.shape
            H, P, N = (NHEADS, HEADDIM, DSTATE)
            G = D_XB // P
            rep = H // G
            zxbcdt = x @ w_in.T
            z, xs, Bs, Cs, dt = jnp.split(zxbcdt, [D_INNER, D_INNER + D_XB, D_INNER + 2 * D_XB, 2 * D_INNER + 2 * D_XB], axis=-1)
            xBC = jnp.concatenate([xs, Bs, Cs], axis=-1)
            conv = jax.lax.conv_general_dilated(xBC.transpose(0, 2, 1), conv_w[:, None, :], (1,), [(DCONV - 1, 0)], feature_group_count=conv_w.shape[0])
            xBC = silu(conv.transpose(0, 2, 1) + conv_b)
            xs, Bs, Cs = jnp.split(xBC, [D_XB, 2 * D_XB], axis=-1)
            dt = jax.nn.softplus(dt + dt_bias)
            A = -jnp.exp(A_log)
            xh = jnp.repeat(xs.reshape(B, L, G, P), rep, axis=2)
            Bh = jnp.repeat(Bs.reshape(B, L, G, N), rep, axis=2)
            Ch = Cs.reshape(B, L, H, N)
            c, Q = (L // CHUNK, CHUNK)
            a = (dt * A).reshape(B, c, Q, H).transpose(0, 1, 3, 2)
            dtc = dt.reshape(B, c, Q, H).transpose(0, 1, 3, 2)
            Xc = xh.reshape(B, c, Q, H, P).transpose(0, 1, 3, 2, 4)
            Bc = Bh.reshape(B, c, Q, H, N).transpose(0, 1, 3, 2, 4)
            Cc = Ch.reshape(B, c, Q, H, N).transpose(0, 1, 3, 2, 4)
            cs = jnp.cumsum(a, axis=-1)
            tri = jnp.tril(jnp.ones((Q, Q), bool))
            Ldec = jnp.where(tri, jnp.exp(cs[..., :, None] - cs[..., None, :]), 0.0)
            Xdt = Xc * dtc[..., None]
            att = jnp.einsum('bchqn,bchkn->bchqk', Cc, Bc) * Ldec
            Yd = jnp.einsum('bchqk,bchkp->bchqp', att, Xdt)
            dec_end = jnp.exp(cs[..., -1:] - cs)
            states = jnp.einsum('bchq,bchqn,bchqp->bchpn', dec_end, Bc, Xdt)
            g = jnp.exp(cs[..., -1])

            def step(S, inp):
                gk, st = inp
                return (gk[:, :, None, None] * S + st, S)
            S0 = jnp.zeros((B, H, P, N), x.dtype)
            _, prev = jax.lax.scan(step, S0, (g.transpose(1, 0, 2), states.transpose(1, 0, 2, 3, 4)))
            prev = prev.transpose(1, 0, 2, 3, 4)
            Yo = jnp.einsum('bchqn,bchpn,bchq->bchqp', Cc, prev, jnp.exp(cs))
            Y = (Yd + Yo).transpose(0, 1, 3, 2, 4).reshape(B, L, H, P)
            Y = Y + D[:, None] * xh
            y = Y.reshape(B, L, D_INNER) * silu(z)
            return y @ w_out.T
        key = jax.random.key(seed)
        ks = jax.random.split(key, 10)
        B, L = (2, 256)
        proj_out = 2 * D_INNER + 2 * D_XB + NHEADS
        conv_dim = 2 * D_XB + D_INNER
        return {'hidden_states': jax.random.normal(ks[0], (B, L, D_MODEL), jnp.float32), 'w_in': jax.random.normal(ks[1], (proj_out, D_MODEL), jnp.float32) * 0.02, 'conv_w': jax.random.normal(ks[2], (conv_dim, DCONV), jnp.float32) * 0.1, 'conv_b': jnp.zeros((conv_dim,), jnp.float32), 'A_log': jnp.log(jnp.arange(1, NHEADS + 1, dtype=jnp.float32)), 'D': jnp.ones((NHEADS,), jnp.float32), 'dt_bias': jax.random.normal(ks[3], (NHEADS,), jnp.float32) * 0.1, 'w_out': jax.random.normal(ks[4], (D_MODEL, D_INNER), jnp.float32) * 0.02, 'ln1_w': jnp.ones((D_MODEL,), jnp.float32), 'ln2_w': jnp.ones((D_MODEL,), jnp.float32), 'gate_w': jax.random.normal(ks[5], (INTER, D_MODEL), jnp.float32) * 0.02, 'up_w': jax.random.normal(ks[6], (INTER, D_MODEL), jnp.float32) * 0.02, 'down_w': jax.random.normal(ks[7], (D_MODEL, INTER), jnp.float32) * 0.02}
    _L0_attn_all = _L0_attn_setup()
    _L0_attn_in = {k: v for k, v in _L0_attn_all.items() if k in ('w_in', 'conv_w', 'conv_b', 'A_log', 'D', 'dt_bias', 'w_out', 'ln1_w', 'ln2_w', 'gate_w', 'up_w', 'down_w')}
    del _L0_attn_all

    def _L0_xattn_setup():
        import jax, jax.numpy as jnp
        import numpy as np
        key = jax.random.key(seed)
        k1, k2 = jax.random.split(key)
        B, Lq, Lk, D = (16, 128, 256, 512)
        query = jax.random.normal(k1, (B, Lq, D), dtype=jnp.float32)
        key_t = jax.random.normal(k2, (B, Lk, D), dtype=jnp.float32)
        return {'query': query, 'key': key_t}
    _L0_xattn_all = _L0_xattn_setup()
    _L0_xattn_in = {k: v for k, v in _L0_xattn_all.items() if k in ()}
    del _L0_xattn_all

    def _L0_ffn_setup():
        import jax, jax.numpy as jnp
        import numpy as np
        NUM_EXPERTS = 4
        HIDDEN = 512
        RANK = 8
        ALPHA = 8.0
        SCALE = ALPHA / RANK
        key = jax.random.key(seed)
        ks = jax.random.split(key, 6)
        B, T, H, E, R = (4, 512, HIDDEN, NUM_EXPERTS, RANK)
        x = jax.random.normal(ks[0], (B, T, H), dtype=jnp.float32)
        W_up = jax.random.normal(ks[1], (H, H), dtype=jnp.float32) / np.sqrt(H)
        gate_w = jax.random.normal(ks[2], (E, H), dtype=jnp.float32) / np.sqrt(H)
        expert_bias = jnp.zeros((E,), dtype=jnp.float32)
        lora_A = jax.random.normal(ks[3], (E, R, H), dtype=jnp.float32) / np.sqrt(H)
        lora_B = jax.random.normal(ks[4], (E, H, R), dtype=jnp.float32) * 0.01
        return {'x': x, 'W_up': W_up, 'gate_w': gate_w, 'expert_bias': expert_bias, 'lora_A': lora_A, 'lora_B': lora_B}
    _L0_ffn_all = _L0_ffn_setup()
    _L0_ffn_in = {k: v for k, v in _L0_ffn_all.items() if k in ('W_up', 'gate_w', 'expert_bias', 'lora_A', 'lora_B')}
    del _L0_ffn_all
    return {'x': x, 'ctx_4096': ctx_4096, 'L0_attn_w_in': _L0_attn_in['w_in'], 'L0_attn_conv_w': _L0_attn_in['conv_w'], 'L0_attn_conv_b': _L0_attn_in['conv_b'], 'L0_attn_A_log': _L0_attn_in['A_log'], 'L0_attn_D': _L0_attn_in['D'], 'L0_attn_dt_bias': _L0_attn_in['dt_bias'], 'L0_attn_w_out': _L0_attn_in['w_out'], 'L0_attn_ln1_w': _L0_attn_in['ln1_w'], 'L0_attn_ln2_w': _L0_attn_in['ln2_w'], 'L0_attn_gate_w': _L0_attn_in['gate_w'], 'L0_attn_up_w': _L0_attn_in['up_w'], 'L0_attn_down_w': _L0_attn_in['down_w'], 'L0_ffn_W_up': _L0_ffn_in['W_up'], 'L0_ffn_gate_w': _L0_ffn_in['gate_w'], 'L0_ffn_expert_bias': _L0_ffn_in['expert_bias'], 'L0_ffn_lora_A': _L0_ffn_in['lora_A'], 'L0_ffn_lora_B': _L0_ffn_in['lora_B']}

def reference(x, ctx_4096, L0_attn_w_in, L0_attn_conv_w, L0_attn_conv_b, L0_attn_A_log, L0_attn_D, L0_attn_dt_bias, L0_attn_w_out, L0_attn_ln1_w, L0_attn_ln2_w, L0_attn_gate_w, L0_attn_up_w, L0_attn_down_w, L0_ffn_W_up, L0_ffn_gate_w, L0_ffn_expert_bias, L0_ffn_lora_A, L0_ffn_lora_B):
    import jax
    import jax.numpy as jnp

    def _L0_attn_ref(hidden_states, w_in, conv_w, conv_b, A_log, D, dt_bias, w_out, ln1_w, ln2_w, gate_w, up_w, down_w):
        import jax, jax.numpy as jnp
        import numpy as np
        D_MODEL = 512
        D_XB = 128
        D_INNER = 512
        HEADDIM = 128
        DSTATE = 128
        NHEADS = D_INNER // HEADDIM
        DCONV = 4
        INTER = 1792
        EPS = 1e-05
        CHUNK = 128

        def rmsnorm(x, w):
            return x * jax.lax.rsqrt(jnp.mean(x * x, axis=-1, keepdims=True) + EPS) * w

        def silu(x):
            return x * jax.nn.sigmoid(x)

        def mamba2(x, w_in, conv_w, conv_b, A_log, D, dt_bias, w_out):
            B, L, _ = x.shape
            H, P, N = (NHEADS, HEADDIM, DSTATE)
            G = D_XB // P
            rep = H // G
            zxbcdt = x @ w_in.T
            z, xs, Bs, Cs, dt = jnp.split(zxbcdt, [D_INNER, D_INNER + D_XB, D_INNER + 2 * D_XB, 2 * D_INNER + 2 * D_XB], axis=-1)
            xBC = jnp.concatenate([xs, Bs, Cs], axis=-1)
            conv = jax.lax.conv_general_dilated(xBC.transpose(0, 2, 1), conv_w[:, None, :], (1,), [(DCONV - 1, 0)], feature_group_count=conv_w.shape[0])
            xBC = silu(conv.transpose(0, 2, 1) + conv_b)
            xs, Bs, Cs = jnp.split(xBC, [D_XB, 2 * D_XB], axis=-1)
            dt = jax.nn.softplus(dt + dt_bias)
            A = -jnp.exp(A_log)
            xh = jnp.repeat(xs.reshape(B, L, G, P), rep, axis=2)
            Bh = jnp.repeat(Bs.reshape(B, L, G, N), rep, axis=2)
            Ch = Cs.reshape(B, L, H, N)
            c, Q = (L // CHUNK, CHUNK)
            a = (dt * A).reshape(B, c, Q, H).transpose(0, 1, 3, 2)
            dtc = dt.reshape(B, c, Q, H).transpose(0, 1, 3, 2)
            Xc = xh.reshape(B, c, Q, H, P).transpose(0, 1, 3, 2, 4)
            Bc = Bh.reshape(B, c, Q, H, N).transpose(0, 1, 3, 2, 4)
            Cc = Ch.reshape(B, c, Q, H, N).transpose(0, 1, 3, 2, 4)
            cs = jnp.cumsum(a, axis=-1)
            tri = jnp.tril(jnp.ones((Q, Q), bool))
            Ldec = jnp.where(tri, jnp.exp(cs[..., :, None] - cs[..., None, :]), 0.0)
            Xdt = Xc * dtc[..., None]
            att = jnp.einsum('bchqn,bchkn->bchqk', Cc, Bc) * Ldec
            Yd = jnp.einsum('bchqk,bchkp->bchqp', att, Xdt)
            dec_end = jnp.exp(cs[..., -1:] - cs)
            states = jnp.einsum('bchq,bchqn,bchqp->bchpn', dec_end, Bc, Xdt)
            g = jnp.exp(cs[..., -1])

            def step(S, inp):
                gk, st = inp
                return (gk[:, :, None, None] * S + st, S)
            S0 = jnp.zeros((B, H, P, N), x.dtype)
            _, prev = jax.lax.scan(step, S0, (g.transpose(1, 0, 2), states.transpose(1, 0, 2, 3, 4)))
            prev = prev.transpose(1, 0, 2, 3, 4)
            Yo = jnp.einsum('bchqn,bchpn,bchq->bchqp', Cc, prev, jnp.exp(cs))
            Y = (Yd + Yo).transpose(0, 1, 3, 2, 4).reshape(B, L, H, P)
            Y = Y + D[:, None] * xh
            y = Y.reshape(B, L, D_INNER) * silu(z)
            return y @ w_out.T
        res = hidden_states
        h = rmsnorm(hidden_states, ln1_w)
        h = res + mamba2(h, w_in, conv_w, conv_b, A_log, D, dt_bias, w_out)
        res = h
        h2 = rmsnorm(h, ln2_w)
        mlp = silu(h2 @ gate_w.T) * (h2 @ up_w.T) @ down_w.T
        return res + mlp

    def _L0_xattn_ref(query, key):
        import jax, jax.numpy as jnp
        import numpy as np
        a = jnp.einsum('bqd,bkd->bqk', query, key)
        e = jax.nn.softmax(a, axis=-1)
        c = jnp.einsum('bqk,bkd->bqd', e, key)
        return c

    def _L0_ffn_ref(x, W_up, gate_w, expert_bias, lora_A, lora_B):
        import jax, jax.numpy as jnp
        import numpy as np
        NUM_EXPERTS = 4
        HIDDEN = 512
        RANK = 8
        ALPHA = 8.0
        SCALE = ALPHA / RANK
        B, T, H = x.shape
        E = gate_w.shape[0]
        x_flat = x.reshape(-1, H)
        logits = x_flat @ gate_w.T + expert_bias
        top1 = jnp.argmax(logits, axis=-1)
        one_hot = jax.nn.one_hot(top1, E, dtype=x_flat.dtype)
        base_out = jnp.einsum('bth,oh->bto', x, W_up)
        z = jnp.einsum('nh,erh->ner', x_flat, lora_A)
        d = jnp.einsum('ner,ehr->neh', z, lora_B) * SCALE
        delta = jnp.einsum('neh,ne->nh', d, one_hot)
        return base_out + delta.reshape(B, T, H)
    x = _layernorm(x + _L0_attn_ref(x, L0_attn_w_in, L0_attn_conv_w, L0_attn_conv_b, L0_attn_A_log, L0_attn_D, L0_attn_dt_bias, L0_attn_w_out, L0_attn_ln1_w, L0_attn_ln2_w, L0_attn_gate_w, L0_attn_up_w, L0_attn_down_w), axis=-1)
    x = _layernorm(x + _L0_xattn_ref(x, ctx_4096), axis=-1)
    x = _layernorm(x + _L0_ffn_ref(x, L0_ffn_W_up, L0_ffn_gate_w, L0_ffn_expert_bias, L0_ffn_lora_A, L0_ffn_lora_B), axis=-1)
    return x

_drawn_inputs = setup_inputs


def setup_inputs(seed=0):
    import zlib

    import numpy as np

    out = dict(_drawn_inputs(seed))
    spreads = {'L0_attn_conv_b': (0.0, 0.621),
     'L0_attn_D': (1.0, 0.6),
     'L0_attn_ln1_w': (1.0, 0.6),
     'L0_attn_ln2_w': (1.0, 0.6),
     'L0_ffn_expert_bias': (0.0, 0.8)}
    factors = {'L0_attn_w_in': 4.526,
     'L0_attn_conv_w': 4.262,
     'L0_attn_A_log': 8.0,
     'L0_attn_dt_bias': 8.0,
     'L0_attn_w_out': 3.241,
     'L0_ffn_gate_w': 3.382,
     'L0_ffn_lora_A': 2.972,
     'L0_ffn_lora_B': 2.912,
     'L0_attn_gate_w': 8.0,
     'L0_attn_up_w': 8.0,
     'L0_attn_down_w': 8.0}
    for name, (base, spread) in spreads.items():
        noise = np.random.default_rng([zlib.crc32(name.encode()), seed]).standard_normal(out[name].shape)
        drawn = base * np.exp(spread * noise) if base else spread * noise
        out[name] = jnp.asarray(drawn.astype(out[name].dtype))
    for name, factor in factors.items():
        out[name] = (out[name] * factor).astype(out[name].dtype)
    return out
```

```python
from contextlib import ExitStack

import concourse.bass as bass
from concourse import mybir

F32 = mybir.dt.float32
F32R = mybir.dt.float32r
BF16 = mybir.dt.bfloat16
ALU = mybir.AluOpType
ACT = mybir.ActivationFunctionType
AX = mybir.AxisListType
LN_EXP = "natural_log_exp_and_others"

P = 128
D = 512
DC = D // P
B = 8
L = 128
TOK = B * L
HALF = TOK // 2
HB = B // 2
H = 4
INTER = 1792
NM = INTER // P
E = 4
RANK = 8
EPS = 1e-5
FUTURE = 1e30

CH = 1024
N_IN = 11
N_CONV = 6
IN_CHUNKS = (N_IN + 1) // 2
OUT_CHUNK = IN_CHUNKS
GU_CHUNK = OUT_CHUNK + 2
LOOP_CHUNK = GU_CHUNK + 2
N_CHUNKS = LOOP_CHUNK + 3 * (NM // 2)
RAW = 3

SEGS = ((0, 6), (6, 8), (8, 11), (11, 14))


def raw_slot(n):
    return (n - LOOP_CHUNK) % RAW


def build(nc, x, ctx, ctxT, wstream, conv_w, conv_b, a_log, d_skip, dt_bias, ln1_w, ln2_w,
          gate_lora, expert_bias, lora_b, out):
    es = ExitStack()
    with es:
        def sb(name, shape, dt=F32):
            return es.enter_context(nc.sbuf_tensor(name, shape, dt))

        def sem(name):
            return es.enter_context(nc.semaphore(name))

        cols = sb("cols", [P, 8192], F32R)
        colsT = cols[:, :].rearrange("p (s c t) -> p s c t", s=2, c=DC)
        hidS = cols[:, 0:4 * NM * P].rearrange("p (b s n) -> p b s n", b=2, s=2)
        x2S = cols[:, 4 * NM * P:8192].rearrange("p (s n) -> p s n", s=2)
        wdS_t = sb("wdS", [P, 2 * NM * D], F32R)
        wdS = wdS_t[:, :].rearrange("p (s n) -> p s n", s=2)
        ringS_t = sb("ringS", [P, 2 * 2 * CH], F32R)
        ringS = ringS_t[:, :].rearrange("p (b s n) -> p b s n", b=2, s=2)
        rows = sb("rows", [P, B, D])
        big = sb("big", [P, NM * TOK])
        raw = sb("raw", [P, RAW, CH])
        tmp = sb("tmp", [P, 7 * D])
        szT = big[:, 0:4096].rearrange("p (h t) -> p h t", h=H)
        cT = big[:, 4096:8192].rearrange("p (h t) -> p h t", h=H)
        xT = big[:, 8192:9216]
        bT = big[:, 9216:10240]
        dI = big[:, 10240:10752].rearrange("p (h q) -> p h q", h=H)
        dec = big[:, 10752:11776].rearrange("p (b h q) -> p b h q", b=2, h=H)
        negcs = big[0:H, 11776:12800]
        spare = big[:, 12800:13312].bitcast(BF16)
        sq_out = spare[:, 0:D]
        future = spare[:, D:2 * D].rearrange("p (h q) -> p h q", h=H)
        ln1r = big[:, 13312:13824]
        ln2r = big[:, 13824:14336]
        hid = big[:, :].rearrange("p (t n) -> p t n", t=B)
        hn = tmp[:, 0:1024].rearrange("p (b n) -> p b n", b=2)
        acc = tmp[:, 1024:2048].rearrange("p (b n) -> p b n", b=2)
        dt_row = tmp[0:H, 2048:3072]
        sel = tmp[0:H, 3072:3584].rearrange("p (h q) -> p h q", h=H)
        u1 = tmp[:, 0:512]
        u2 = tmp[:, 512:1536].rearrange("p (b n) -> p b n", b=2)
        u3 = tmp[:, 1536:2048]
        qT = tmp[:, 2048:2560]
        x2T = tmp[:, 2560:3072]
        ex = tmp[:, 3072:3200]
        exT = tmp[:, 3200:3328]
        zm = tmp[:, 3328:3456]
        zmT = tmp[0:E * RANK, 3456:3584]
        xb = sb("xb", [P, 2, P + 2 * H])
        ident = sb("ident", [P, P])
        identb = sb("identb", [P, P], BF16)
        ones = sb("ones", [H, P])
        epsc = sb("epsc", [P, 1])
        onec = sb("onec", [P, 1])
        cw = sb("cw", [P, N_CONV, 4])
        cb = sb("cb", [P, N_CONV])
        dsk = sb("dsk", [P, H])
        dtb = sb("dtb", [H, 1])
        alog = sb("alog", [H, 1])
        expa = sb("expa", [H, 1])
        ga = sb("ga", [P, DC, E + E * RANK])
        lb = sb("lb", [E * RANK, D])
        eb = sb("eb", [P, E])
        codes = sb("codes", [P, E])
        ssq = sb("ssq", [P, 2, B])
        rst = sb("rst", [P, 2, B])
        stats = sb("stats", [P, 3, 6])
        mv = sb("mv", [P, 3, 2])
        lrs = sb("lrs", [P, 3])
        sm = sb("sm", [P, 3])
        lg = sb("lg", [P, 3, E])
        gm = sb("gm", [P, 2])

        bank = [es.enter_context(nc.psum_tensor(f"bank{i}", [P, D], F32)) for i in range(8)]

        x_in = [sem(f"x_in{t}") for t in range(B)]
        const_in = sem("const_in")
        ln1_in = sem("ln1_in")
        raw_in = [sem(f"raw_in{i}") for i in range(RAW)]
        ctx_in = [sem(f"ctx_in{i}") for i in range(2)]
        stored = sem("stored")
        pool_setup = sem("pool_setup")
        zm_clear = sem("zm_clear")
        vec_setup = sem("vec_setup")
        expa_ok = sem("expa_ok")
        w_hi = sem("w_hi")
        w_lo = sem("w_lo")
        ring_lo = sem("ring_lo")
        sq1, lr1, rs1, hn1 = sem("sq1"), sem("lr1"), sem("rs1"), sem("hn1")
        hT_ps, hT_hi, hT_lo = sem("hT_ps"), sem("hT_hi"), sem("hT_lo")
        ip_done, ip_used, z_done = sem("ip_done"), sem("ip_used"), sem("z_done")
        sp_step, sp_exp, sp_ln = sem("sp_step"), sem("sp_exp"), sem("sp_ln")
        dt_ok, a_ok, cs_ok = sem("dt_ok"), sem("a_ok"), sem("cs_ok")
        cv_init, cv_tap, cv_done = sem("cv_init"), sem("cv_tap"), sem("cv_done")
        s1_done, xb_ok, dec_exp = sem("s1_done"), sem("xb_ok"), sem("dec_exp")
        att_ok, attd_ok, y_ps, y_gated = sem("att_ok"), sem("attd_ok"), sem("y_ps"), sem("y_gated")
        y_hi, y_lo = sem("y_hi"), sem("y_lo")
        op_done, h_ok, hx_ok = sem("op_done"), sem("h_ok"), sem("hx_ok")
        sq2, lr2, rs2, hn2 = sem("sq2"), sem("lr2"), sem("rs2"), sem("hn2")
        h2_ps, h2_hi, h2_lo = sem("h2_ps"), sem("h2_hi"), sem("h2_lo")
        gu_done, sg_ok, hid_ok = sem("gu_done"), sem("sg_ok"), sem("hid_ok")
        hid_hi, hid_lo, down_ps = sem("hid_hi"), sem("hid_lo"), sem("down_ps")
        ln_u, ln_st, ln_mv, ln_log, ln_rs, ln_out = (
            [sem(f"ln{i}_{what}") for i in (1, 2, 3)] for what in ("u", "st", "mv", "log", "rs", "out"))
        q_ps, q_ok, sc_ps, mx_ok, ex_ok = sem("q_ps"), sem("q_ok"), sem("sc_ps"), sem("mx_ok"), sem("ex_ok")
        rinv_ok, exT_ps, exT_ok, pv_ps = sem("rinv_ok"), sem("exT_ps"), sem("exT_ok"), sem("pv_ps")
        x2_ps, x2_ok, x2_hi, x2_lo = sem("x2_ps"), sem("x2_ok"), sem("x2_hi"), sem("x2_lo")
        route_ps, lg_step, zm_ok = sem("route_ps"), sem("lg_step"), sem("zm_ok")
        zmT_ps, zmT_ok, ffn_ps = sem("zmT_ps"), sem("zmT_ok"), sem("ffn_ps")

        block = es.enter_context(nc.Block())

        def tok(b):
            return bass.ts(b, L)

        def half(hf):
            return bass.ts(hf, HALF)

        def blocks(ap):
            return ap.rearrange("p (c q) -> p c q", c=DC)

        def context(t):
            return (big[:, bass.ds(t * (NM * P), D)], big[:, bass.ds(t * (NM * P) + D, D)])


        @block.sync
        def _(sp):
            def load_chunk(n):
                sp.dma_start(raw[:, raw_slot(n), :], wstream[n]).then_inc(raw_in[raw_slot(n)], 16)

            for t in range(2):
                sp.dma_start(rows[:, t, :], x[t]).then_inc(x_in[t], 16)
            sp.dma_start(ln1r, ln1_w.partition_broadcast(P)).then_inc(ln1_in, 16)
            load_chunk(0)
            for t in range(2, HB):
                sp.dma_start(rows[:, t, :], x[t]).then_inc(x_in[t], 16)
            for dst, src in ((alog[:, :], a_log), (dtb[:, :], dt_bias), (cw[:, :, :], conv_w),
                             (cb[:, :], conv_b), (dsk[:, :], d_skip.partition_broadcast(P)),
                             (ln2r, ln2_w.partition_broadcast(P)), (ga[:, :, :], gate_lora),
                             (lb[:, :], lora_b), (eb[:, :], expert_bias.partition_broadcast(P))):
                sp.dma_start(dst, src).then_inc(const_in, 16)
            for t in range(HB, B):
                sp.dma_start(rows[:, t, :], x[t]).then_inc(x_in[t], 16)
            load_chunk(1)
            load_chunk(2)
            for n in range(RAW, LOOP_CHUNK):
                sp.wait_ge(w_lo, n - RAW + 1)
                load_chunk(n)
            for i in range(RAW):
                sp.wait_ge(w_lo, LOOP_CHUNK + i - RAW + 1)
                load_chunk(LOOP_CHUNK + i)
            with sp.Fori(1, NM // 2) as j:
                chunks = [sp.snap(3 * j + (LOOP_CHUNK + i)) for i in range(RAW)]
                for i in range(RAW):
                    if i < 2:
                        sp.wait_ge(ring_lo, 2 * j + (i - 1))
                    else:
                        sp.wait_ge(w_lo, j + LOOP_CHUNK)
                    sp.dma_start(raw[:, i, :], wstream[bass.ds(chunks[i], 1)]
                                 .rearrange("a p n -> (a p) n")).then_inc(raw_in[i], 16)
            for t in range(B):
                sp.wait_ge(hid_lo, t + 1)
                if t >= 2:
                    sp.wait_ge(ctx_in[t % 2], 32 * (t // 2))
                keyT, key = context(t)
                sp.dma_start(keyT, ctxT[t]).then_inc(ctx_in[t % 2], 16)
                sp.dma_start(key, ctx[t]).then_inc(ctx_in[t % 2], 16)
            sp.wait_ge(stored, 16 * B)

        @block.gpsimd
        def _(pool):
            pool.memset(ident[:, :], 0.0).then_inc(pool_setup, 1)
            pool.memset(sel, 1.0).then_inc(pool_setup, 1)
            pool.wait_ge(pool_setup, 2)
            pool.affine_select(out=ident[:, :], in_=ident[:, :], compare_op=ALU.not_equal, fill=1.0,
                               base=0, pattern=[[-1, P]], channel_multiplier=1).then_inc(pool_setup, 1)
            pool.affine_select(out=sel, in_=sel, compare_op=ALU.is_equal, fill=0.0,
                               base=0, pattern=[[-1, H], [0, P]], channel_multiplier=1).then_inc(pool_setup, 1)
            pool.memset(future, 0.0).then_inc(pool_setup, 1)
            pool.wait_ge(pool_setup, 5)
            pool.tensor_copy(identb[:, :], ident[:, :]).then_inc(pool_setup, 1)
            pool.affine_select(out=future, in_=future, compare_op=ALU.is_ge, fill=FUTURE, base=0,
                               pattern=[[0, H], [1, L]], channel_multiplier=-1).then_inc(pool_setup, 1)
            for e in range(E):
                mm = pool.memset(codes[:, e:e + 1], float(E - e))
            mm.then_inc(pool_setup, 1)

            def lo_part(n, dst, hi):
                pool.wait_ge(w_hi, n + 1)
                pool.tensor_tensor(dst, raw[:, raw_slot(n), :], hi.bitcast(F32), ALU.subtract).then_inc(w_lo, 1)

            for n in range(IN_CHUNKS):
                lo_part(n, ringS[:, n % 2, 1, :], ringS[:, n % 2, 0, :])
            for i in range(2):
                lo_part(OUT_CHUNK + i, wdS[:, 1, bass.ts(i, CH)], wdS[:, 0, bass.ts(i, CH)])

            def skip(b):
                d = dec[:, b % 2, :, :]
                if b == 0:
                    pool.wait_ge(vec_setup, 2)
                pool.wait_ge(att_ok, H * (b + 1))
                pool.tensor_tensor(d, d, dI, ALU.add).then_inc(attd_ok, 1)

            def residual(b):
                pool.wait_ge(h_ok, b + 1)
                pool.tensor_tensor(rows[:, b, :], rows[:, b, :], acc[:, b % 2, :], ALU.add).then_inc(hx_ok, 1)

            skip(0)
            skip(1)
            for b in range(B + 1):
                if b + 2 < B:
                    skip(b + 2)
                if b == 2:
                    for i in range(2):
                        lo_part(GU_CHUNK + i, ringS[:, i, 1, :], ringS[:, i, 0, :])
                if b >= 1:
                    residual(b - 1)
            pool.memset(zm, 0.0).then_inc(zm_clear, 1)
            with pool.Fori(0, NM // 2) as j:
                pool.wait_ge(w_hi, 3 * j + (LOOP_CHUNK + 3))
                pool.tensor_tensor(wdS_t[:, bass.ds(j * CH + NM * D, CH)], raw[:, 2, :],
                                   wdS_t[:, bass.ds(j * CH, CH)].bitcast(F32), ALU.subtract).then_inc(w_lo, 1)

        IPB = 3
        N_DVE_IP = 2 + 2 * N_CONV

        def three_pass(pe, ps, a_hi, a_lo, b_hi, b_lo, first, last):
            pe.matmul(ps, a_hi, b_lo, start=first, stop=False)
            pe.matmul(ps, a_hi, b_hi, start=False, stop=False)
            return pe.matmul(ps, a_lo, b_hi, start=False, stop=last)

        @block.tensor
        def _(pe):
            def turn_h(t):
                pe.wait_ge(hn1, t + 1)
                if t >= 2:
                    pe.wait_ge(hT_lo, t - 1)
                for c in range(DC):
                    mm = pe.transpose(bank[t % 2][:, bass.ts(c, P)], hn[:, t % 2, bass.ts(c, P)], ident[:, :])
                mm.then_inc(hT_ps, 1)

            def in_proj(m, hf):
                n = 2 * m + hf
                pe.wait_ge(w_lo, m // 2 + 1)
                pe.wait_ge(hT_lo, HB * (hf + 1))
                before = n - IPB
                if 0 <= before < N_DVE_IP:
                    pe.wait_ge(ip_used, before + 1)
                elif before >= N_DVE_IP:
                    pe.wait_ge(z_done, before - N_DVE_IP + 1)
                w = ringS[:, (m // 2) % 2, :, bass.ts(m % 2, D)]
                for c in range(DC):
                    mm = three_pass(pe, bank[2 + n % IPB][:, :], w[:, 0, bass.ts(c, P)], w[:, 1, bass.ts(c, P)],
                                    colsT[:, 0, c, half(hf)], colsT[:, 1, c, half(hf)], c == 0, c == DC - 1)
                mm.then_inc(ip_done, 1)

            def scores_of(b):
                pe.wait_ge(cs_ok, b + 1)
                pe.wait_ge(cv_done, 2 * N_CONV - 1 + b // HB)
                if b >= 2:
                    pe.wait_ge(dec_exp, H * (b - 1))
                if b >= 1:
                    pe.wait_ge(xb_ok, b)
                    pe.wait_ge(att_ok, H * b)
                pe.matmul(bank[b % 2][:, :], identb[:, :], future, start=True, stop=False)
                for h in range(H):
                    pe.matmul(bank[b % 2][:, bass.ts(h, L)], sel[:, h, :], negcs[:, tok(b)],
                              start=False, stop=(h == H - 1))
                pe.transpose(bank[5][:, 0:P], xT[:, tok(b)], ident[:, :])
                pe.transpose(bank[5][:, P:P + H], negcs[:, tok(b)], ident[0:H, 0:H])
                pe.transpose(bank[5][:, P + H:P + 2 * H], dt_row[:, tok(b)], ident[0:H, 0:H])
                pe.matmul(bank[6][:, :], bT[:, tok(b)], cT[:, :, tok(b)], start=True, stop=True).then_inc(s1_done, 1)

            def y_of(b):
                pe.wait_ge(attd_ok, b + 1)
                pe.wait_ge(xb_ok, b + 1)
                if b >= 1:
                    pe.wait_ge(y_gated, b)
                pe.matmul(bank[7][:, :], xb[:, b % 2, 0:P], dec[:, b % 2, :, :], start=True, stop=True) \
                    .then_inc(y_ps, 1)

            def out_proj(b):
                if b == 0:
                    pe.wait_ge(w_lo, OUT_CHUNK + 2)
                    pe.wait_ge(z_done, 2 * H)
                pe.wait_ge(y_lo, b + 1)
                if b >= 2:
                    pe.wait_ge(h_ok, b - 1)
                for c in range(DC):
                    mm = three_pass(pe, bank[2 + b % 2][:, :], colsT[:, 0, c, tok(b)], colsT[:, 1, c, tok(b)],
                                    wdS[:, 0, bass.ts(c, D)], wdS[:, 1, bass.ts(c, D)], c == 0, c == DC - 1)
                mm.then_inc(op_done, 1)

            def turn_h2(b):
                pe.wait_ge(hn2, b + 1)
                if b >= 1:
                    pe.wait_ge(h2_lo, b)
                for c in range(DC):
                    mm = pe.transpose(bank[4][:, bass.ts(c, P)], acc[:, b % 2, bass.ts(c, P)], ident[:, :])
                mm.then_inc(h2_ps, 1)

            def gate_up(par, hf):
                for g in range(2):
                    for c in range(DC):
                        col = g * D + c * P
                        mm = three_pass(pe, bank[4 * par + 2 * hf + g][:, :],
                                        ringS[:, par, 0, col:col + P], ringS[:, par, 1, col:col + P],
                                        colsT[:, 0, c, half(hf)], colsT[:, 1, c, half(hf)], c == 0, c == DC - 1)
                mm.then_inc(gu_done, 1)

            pe.wait_ge(pool_setup, 8)
            for t in range(HB):
                turn_h(t)
            in_proj(0, 0)
            for t in range(HB, B):
                turn_h(t)
            in_proj(0, 1)
            for m in range(1, N_CONV + 3):
                for hf in range(2):
                    in_proj(m, hf)
                if m == N_CONV + 1:
                    scores_of(0)
            scores_of(1)
            for m in range(N_CONV + 3, N_IN):
                for hf in range(2):
                    in_proj(m, hf)
            for b in range(B + 3):
                if b < B:
                    y_of(b)
                if b + 2 < B:
                    scores_of(b + 2)
                if 1 <= b <= B:
                    out_proj(b - 1)
                if b >= 3:
                    turn_h2(b - 3)
                if b == B:
                    pe.wait_ge(w_lo, LOOP_CHUNK)
                    gate_up(0, 0)
            pe.wait_ge(h2_lo, B)
            gate_up(1, 0)
            gate_up(0, 1)
            gate_up(1, 1)
            with pe.Fori(1, NM // 2) as j:
                for hf in range(2):
                    for par in range(2):
                        if hf == 0:
                            pe.wait_ge(ring_lo, 2 * j + (par - 1))
                        pe.wait_ge(hid_ok, 4 * j + (2 * hf + par - 3))
                        gate_up(par, hf)

            def down(t, par, seg, first_use):
                k0, k1 = SEGS[seg]
                if k0 == 0:
                    pe.wait_ge(hid_lo, t + 1)
                    if not first_use:
                        pe.wait_ge(ln_u[0], t - 1)
                for k in range(k0, k1):
                    mm = three_pass(pe, bank[par][:, :], hidS[:, par, 0, bass.ts(k, P)],
                                    hidS[:, par, 1, bass.ts(k, P)], wdS[:, 0, bass.ts(k, D)],
                                    wdS[:, 1, bass.ts(k, D)], k == 0, k == NM - 1)
                if k1 == NM:
                    mm.then_inc(down_ps, 1)

            def turn_x1(t):
                pe.wait_ge(ln_out[0], t + 1)
                for c in range(DC):
                    mm = pe.transpose(bank[2][:, bass.ts(c, P)], u1[:, bass.ts(c, P)], ident[:, :])
                mm.then_inc(q_ps, 1)

            def attend(t, par):
                pe.wait_ge(q_ok, t + 1)
                pe.wait_ge(ctx_in[par], 16 * (t + 2 - par))
                keyT, _ = context(t)
                for c in range(DC):
                    mm = pe.matmul(bank[4][:, 0:P], qT[:, bass.ts(c, P)], blocks(keyT)[:, c, :],
                                   start=(c == 0), stop=(c == DC - 1))
                mm.then_inc(sc_ps, 1)

            def turn_ex(t):
                pe.wait_ge(ex_ok, t + 1)
                pe.transpose(bank[4][:, P:2 * P], ex, ident[:, :]).then_inc(exT_ps, 1)

            def mix(t):
                pe.wait_ge(exT_ok, t + 1)
                _, key = context(t)
                pe.matmul(bank[5][:, :], exT, key, start=True, stop=True).then_inc(pv_ps, 1)

            def turn_x2(t, par):
                pe.wait_ge(ln_out[1], t + 1)
                for c in range(DC):
                    mm = pe.transpose(bank[3][:, bass.ts(c, P)], u2[:, par, bass.ts(c, P)], ident[:, :])
                mm.then_inc(x2_ps, 1)

            def route_and_base(t, first_use):
                pe.wait_ge(x2_ok, t + 1)
                for c in range(DC):
                    mm = pe.matmul(bank[7][:, 0:E + E * RANK], x2T[:, bass.ts(c, P)], ga[:, c, :],
                                   start=(c == 0), stop=(c == DC - 1))
                mm.then_inc(route_ps, 1)
                pe.wait_ge(x2_lo, t + 1)
                if not first_use:
                    pe.wait_ge(ln_u[2], t)
                for c in range(DC):
                    three_pass(pe, bank[6][:, :], x2S[:, 0, bass.ts(c, P)], x2S[:, 1, bass.ts(c, P)],
                               ringS[:, c // 2, 0, bass.ts(c % 2, D)], ringS[:, c // 2, 1, bass.ts(c % 2, D)],
                               c == 0, False)

            def turn_z(t):
                pe.wait_ge(zm_ok, t + 1)
                pe.transpose(bank[7][:, P:2 * P], zm, ident[:, :]).then_inc(zmT_ps, 1)

            def lora(t):
                pe.wait_ge(zmT_ok, t + 1)
                pe.matmul(bank[6][:, :], zmT, lb[:, :], start=False, stop=True).then_inc(ffn_ps, 1)

            def tail(t, par, d=True, a=True, f=True, first_d=False, first_f=False):
                if d:
                    down(t, par, 0, first_d)
                if a:
                    turn_x1(t - 1)
                if f:
                    turn_x2(t - 2, par)
                if d:
                    down(t, par, 1, first_d)
                if a:
                    attend(t - 1, 1 - par)
                if f:
                    route_and_base(t - 2, first_f)
                if a:
                    turn_ex(t - 1)
                if d:
                    down(t, par, 2, first_d)
                if f:
                    turn_z(t - 2)
                if a:
                    mix(t - 1)
                if d:
                    down(t, par, 3, first_d)
                if f:
                    lora(t - 2)

            pe.wait_ge(w_lo, LOOP_CHUNK + NM // 2)
            pe.wait_ge(ring_lo, NM)
            tail(0, 0, a=False, f=False, first_d=True)
            tail(1, 1, f=False, first_d=True)
            tail(2, 0, first_f=True)
            with pe.Fori(1, B // 2 - 1) as j:
                tail(2 * j + 1, 1)
                tail(2 * j + 2, 0)
            tail(B - 1, 1)
            tail(B, 0, d=False)
            tail(B + 1, 1, d=False, a=False)

        @block.scalar
        def _(act):
            def hi_part(n, dst):
                landed = sum(raw_slot(i) == raw_slot(n) for i in range(n + 1))
                act.wait_ge(raw_in[raw_slot(n)], 16 * landed)
                act.activation(dst, raw[:, raw_slot(n), :], ACT.Copy).then_inc(w_hi, 1)

            def ring_hi(n):
                if n >= 2:
                    act.wait_ge(ip_done, 4 * (n - 1))
                hi_part(n, ringS[:, n % 2, 0, :])

            def rms(i, t, src, squared, logged, done):
                s, r = ssq[:, i, t:t + 1], rst[:, i, t:t + 1]
                act.activation(sq_out, src, ACT.Square, accum_out=s).then_inc(squared, 1)
                act.wait_ge(squared, t + 1)
                act.activation(r, s, ACT.Ln, bias=epsc[:, :], scale=1.0 / D).then_inc(logged, 1)
                act.wait_ge(logged, t + 1)
                act.activation(r, r, ACT.Exp, scale=-0.5).then_inc(done, 1)

            def norm1(t):
                act.wait_ge(x_in[t], 16)
                if t == 0:
                    act.wait_ge(vec_setup, 1)
                rms(0, t, rows[:, t, :], sq1, lr1, rs1)

            def hi_of_hT(t):
                act.wait_ge(hT_ps, t + 1)
                act.activation(colsT[:, 0, :, tok(t)], blocks(bank[t % 2][:, :]), ACT.Copy).then_inc(hT_hi, 1)

            def softplus(hf):
                v = negcs[:, half(hf)]
                act.wait_ge(sp_step, 3 * (hf + 1))
                act.activation(v, v, ACT.Exp).then_inc(sp_exp, 1)
                act.wait_ge(sp_exp, hf + 1)
                act.activation(v, v, ACT.Ln, bias=onec[0:H, :]).then_inc(sp_ln, 1)

            def conv_last_tap(i):
                m = i // 2
                act.wait_ge(ip_done, 2 + i + 1)
                if i >= 2:
                    act.wait_ge(cv_done, i - 1)
                act.activation(acc[:, i % 2, :], bank[2 + (2 + i) % IPB][:, :], ACT.Identity,
                               bias=cb[:, m:m + 1], scale=cw[:, m, 3:4]).then_inc(cv_init, 1)

            def conv_silu(i):
                m, hf = i // 2, i % 2
                act.wait_ge(cv_tap, 3 * (i + 1))
                dst = xT[:, half(hf)] if m == 0 else bT[:, half(hf)] if m == 1 else cT[:, m - 2, half(hf)]
                act.activation(dst, acc[:, i % 2, :], ACT.Silu).then_inc(cv_done, 1)

            def z_silu(i):
                n = N_DVE_IP + i
                act.wait_ge(ip_done, n + 1)
                act.activation(szT[:, i // 2, half(i % 2)], bank[2 + n % IPB][:, :], ACT.Silu).then_inc(z_done, 1)

            def decay(b):
                act.wait_ge(s1_done, b + 1)
                if b >= 2:
                    act.wait_ge(y_ps, b - 1)
                act.activation(xb[:, b % 2, :], bank[5][:, 0:P + 2 * H], ACT.Copy).then_inc(xb_ok, 1)
                act.wait_ge(xb_ok, b + 1)
                for h in range(H):
                    act.activation(dec[:, b % 2, h, :], bank[b % 2][:, bass.ts(h, L)], ACT.Exp,
                                   bias=xb[:, b % 2, P + h:P + h + 1], scale=-1.0).then_inc(dec_exp, 1)

            def hi_of_y(b):
                act.wait_ge(y_gated, b + 1)
                act.activation(colsT[:, 0, :, tok(b)], blocks(hn[:, b % 2, :]), ACT.Copy).then_inc(y_hi, 1)

            def norm2(b):
                act.wait_ge(h_ok, b + 1)
                rms(1, b, acc[:, b % 2, :], sq2, lr2, rs2)

            def hi_of_h2(b):
                act.wait_ge(h2_ps, b + 1)
                act.activation(colsT[:, 0, :, tok(b)], blocks(bank[4][:, :]), ACT.Copy).then_inc(h2_hi, 1)

            act.preload_act_table_set(LN_EXP)
            norm1(0)
            norm1(1)
            hi_part(0, ringS[:, 0, 0, :])
            for t in range(2, B):
                hi_of_hT(t - 2)
                norm1(t)
            for t in range(B - 2, B):
                hi_of_hT(t)
            act.wait_ge(const_in, 16 * 9)
            act.activation(expa[:, :], alog[:, :], ACT.Exp).then_inc(expa_ok, 1)
            ring_hi(1)
            softplus(0)
            softplus(1)
            for i in range(2 * N_CONV):
                conv_last_tap(i)
                if i >= 1:
                    conv_silu(i - 1)
                if i % 4 == 1:
                    ring_hi(2 + i // 4)
            conv_silu(2 * N_CONV - 1)
            z_silu(0)
            z_silu(1)
            ring_hi(IN_CHUNKS - 1)
            act.preload_act_table_set(LN_EXP)
            decay(0)
            decay(1)
            for i in range(2):
                hi_part(OUT_CHUNK + i, wdS[:, 0, bass.ts(i, CH)])
            for i in range(2, 2 * H):
                z_silu(i)
            act.preload_act_table_set(LN_EXP)
            for b in range(B + 3):
                if b < B:
                    hi_of_y(b)
                if b + 2 < B:
                    decay(b + 2)
                if b == 1:
                    for i in range(2):
                        act.wait_ge(ip_done, 2 * N_IN)
                        hi_part(GU_CHUNK + i, ringS[:, i, 0, :])
                if b >= 3:
                    hi_of_h2(b - 3)
                if 1 <= b <= B:
                    norm2(b - 1)

            def sg(v, par, hf, first_use):
                act.wait_ge(gu_done, v + 1)
                if not first_use:
                    act.wait_ge(hid_ok, v - 1)
                act.activation(hn[:, par, :], bank[4 * par + 2 * hf][:, :], ACT.Silu).then_inc(sg_ok, 1)

            landed = [sum(raw_slot(n) == i for n in range(LOOP_CHUNK)) for i in range(RAW)]

            def pair(j, first_use):
                sg(4 * j, 0, 0, first_use)
                sg(4 * j + 1, 1, 0, first_use)
                sg(4 * j + 2, 0, 1, False)
                act.wait_ge(raw_in[0], 16 * j + 16 * (landed[0] + 1))
                act.activation(ringS[:, 0, 0, :], raw[:, 0, :], ACT.Copy).then_inc(w_hi, 1)
                sg(4 * j + 3, 1, 1, False)
                act.wait_ge(raw_in[1], 16 * j + 16 * (landed[1] + 1))
                act.activation(ringS[:, 1, 0, :], raw[:, 1, :], ACT.Copy).then_inc(w_hi, 1)
                act.wait_ge(raw_in[2], 16 * j + 16 * (landed[2] + 1))
                act.activation(wdS_t[:, bass.ds(j * CH, CH)], raw[:, 2, :], ACT.Copy).then_inc(w_hi, 1)

            pair(0, True)
            with act.Fori(1, NM // 2) as j:
                pair(j, False)

            def split_hid(t, par, first_use=False):
                if not first_use:
                    act.wait_ge(down_ps, t - 1)
                act.activation(hidS[:, par, 0, :], big[:, bass.ds(t * (NM * P), NM * P)], ACT.Copy) \
                    .then_inc(hid_hi, 1)

            def rstd(i, t):
                act.wait_ge(ln_mv[i], t + 1)
                act.activation(lrs[:, i:i + 1], mv[:, i, 1:2], ACT.Ln, bias=epsc[:, :]).then_inc(ln_log[i], 1)
                act.wait_ge(ln_log[i], t + 1)
                act.activation(lrs[:, i:i + 1], lrs[:, i:i + 1], ACT.Exp, scale=-0.5).then_inc(ln_rs[i], 1)

            def store(t):
                act.wait_ge(ln_out[2], t + 1)
                act.dma_start(out[bass.ds(t, 1)].rearrange("a p n -> (a p) n"), u3).then_inc(stored, 16)

            def tail(t, par, a=True, f=True, g=True, split=True, first_split=False):
                if a:
                    rstd(0, t - 1)
                if g:
                    rstd(2, t - 3)
                if split:
                    split_hid(t + 1, 1 - par, first_split)
                if a:
                    act.wait_ge(q_ps, t)
                    act.activation(qT, bank[2][:, :], ACT.Copy).then_inc(q_ok, 1)
                if f:
                    act.wait_ge(x2_ps, t - 1)
                    act.activation(x2T, bank[3][:, :], ACT.Copy).then_inc(x2_ok, 1)
                if g:
                    store(t - 3)
                if a:
                    act.wait_ge(mx_ok, t)
                    act.activation(ex, bank[4][:, 0:P], ACT.Exp, bias=sm[:, 0:1], accum_out=sm[:, 1:2]) \
                        .then_inc(ex_ok, 1)
                    act.wait_ge(exT_ps, t)
                    act.activation(exT, bank[4][:, P:2 * P], ACT.Copy).then_inc(exT_ok, 1)
                if f:
                    act.wait_ge(zmT_ps, t - 1)
                    act.activation(zmT, bank[7][0:E * RANK, P:2 * P], ACT.Copy).then_inc(zmT_ok, 1)
                if a:
                    rstd(1, t - 1)

            act.preload_act_table_set(LN_EXP)
            act.wait_ge(hid_ok, 2 * NM)
            split_hid(0, 0, True)
            tail(0, 0, a=False, f=False, g=False, first_split=True)
            tail(1, 1, f=False, g=False)
            tail(2, 0, g=False)
            with act.Fori(1, B // 2 - 1) as j:
                tail(2 * j + 1, 1)
                tail(2 * j + 2, 0)
            tail(B - 1, 1, split=False)
            tail(B, 0, split=False)
            tail(B + 1, 1, a=False, split=False)
            tail(B + 2, 0, a=False, f=False, split=False)

        @block.vector
        def _(v):
            v.memset(epsc[:, :], EPS)
            v.memset(ones[:, :], 1.0)
            v.memset(onec[:, :], 1.0).then_inc(vec_setup, 1)

            def norm1(t):
                v.wait_ge(rs1, t + 1)
                if t == 0:
                    v.wait_ge(ln1_in, 16)
                if t >= 2:
                    v.wait_ge(hT_ps, t - 1)
                v.scalar_tensor_tensor(out=hn[:, t % 2, :], in0=rows[:, t, :], scalar=rst[:, 0, t:t + 1],
                                       in1=ln1r, op0=ALU.mult, op1=ALU.mult).then_inc(hn1, 1)

            def low(t, src, hi_ready, done):
                v.wait_ge(hi_ready, t + 1)
                v.tensor_tensor(colsT[:, 1, :, tok(t)], blocks(src), colsT[:, 0, :, tok(t)].bitcast(F32),
                                ALU.subtract).then_inc(done, 1)

            for t in range(B):
                norm1(t)
                if t >= 1:
                    low(t - 1, bank[(t - 1) % 2][:, :], hT_hi, hT_lo)
            low(B - 1, bank[(B - 1) % 2][:, :], hT_hi, hT_lo)

            def softplus_in(hf):
                dst, n = negcs[:, half(hf)], bank[2 + hf][0:H, :]
                v.wait_ge(ip_done, hf + 1)
                if hf == 0:
                    v.wait_ge(const_in, 16 * 9)
                v.tensor_scalar(dt_row[:, half(hf)], n, dtb[:, 0:1], 0.0, ALU.add, ALU.max).then_inc(sp_step, 1)
                v.tensor_scalar(dst, n, dtb[:, 0:1], None, ALU.add).then_inc(sp_step, 1)
                v.wait_ge(sp_step, 3 * hf + 2)
                v.scalar_tensor_tensor(out=dst, in0=dst, scalar=-1.0, in1=dst, op0=ALU.mult, op1=ALU.min) \
                    .then_inc(sp_step, 1)
                v.sem_inc(ip_used, 1)

            def time_steps(hf):
                h_ = half(hf)
                v.wait_ge(sp_ln, hf + 1)
                v.tensor_tensor(dt_row[:, h_], dt_row[:, h_], negcs[:, h_], ALU.add).then_inc(dt_ok, 1)
                v.wait_ge(dt_ok, hf + 1)
                v.wait_ge(expa_ok, 1)
                v.tensor_scalar(negcs[:, h_], dt_row[:, h_], expa[:, 0:1], None, ALU.mult).then_inc(a_ok, 1)
                v.wait_ge(a_ok, hf + 1)
                for b in range(HB * hf, HB * (hf + 1)):
                    v.tensor_tensor_scan(negcs[:, tok(b)], ones[:, :], negcs[:, tok(b)], 0.0,
                                         ALU.mult, ALU.add).then_inc(cs_ok, 1)

            def conv_taps(i):
                m = i // 2
                src = bank[2 + (2 + i) % IPB][:, :].rearrange("p (b q) -> p b q", b=HB)
                dst = acc[:, i % 2, :].rearrange("p (b q) -> p b q", b=HB)
                v.wait_ge(cv_init, i + 1)
                for s in range(1, 4):
                    if s > 1:
                        v.wait_ge(cv_tap, 3 * i + s - 1)
                    mm = v.scalar_tensor_tensor(out=dst[:, :, s:L], in0=src[:, :, 0:L - s],
                                                scalar=cw[:, m, 3 - s:4 - s], in1=dst[:, :, s:L],
                                                op0=ALU.mult, op1=ALU.add).then_inc(cv_tap, 1)
                v.wait_ge(cv_tap, 3 * i + 3)
                v.sem_inc(ip_used, 1)

            softplus_in(0)
            softplus_in(1)
            for h in range(H):
                if h == 0:
                    v.wait_ge(pool_setup, 8)
                mm = v.tensor_scalar(dI[:, h, :], ident[:, :], dsk[:, h:h + 1], None, ALU.mult)
            mm.then_inc(vec_setup, 1)
            for i in range(2 * N_CONV):
                conv_taps(i)
                if i == 1:
                    time_steps(0)
                if i == 3:
                    time_steps(1)

            def att(b):
                v.wait_ge(dec_exp, H * (b + 1))
                for h in range(H):
                    v.scalar_tensor_tensor(out=dec[:, b % 2, h, :], in0=bank[6][:, bass.ts(h, L)],
                                           scalar=xb[:, b % 2, P + H + h:P + H + h + 1],
                                           in1=dec[:, b % 2, h, :], op0=ALU.mult, op1=ALU.mult).then_inc(att_ok, 1)

            def gate_y(b):
                v.wait_ge(y_ps, b + 1)
                if b == 0:
                    v.wait_ge(z_done, 2 * H)
                v.tensor_tensor(blocks(hn[:, b % 2, :]), blocks(bank[7][:, :]), szT[:, :, tok(b)], ALU.mult) \
                    .then_inc(y_gated, 1)

            def add_h(b):
                v.wait_ge(op_done, b + 1)
                if b >= 2:
                    v.wait_ge(h2_ps, b - 1)
                v.tensor_tensor(acc[:, b % 2, :], bank[2 + b % 2][:, :], rows[:, b, :], ALU.add).then_inc(h_ok, 1)

            def norm2(b):
                v.wait_ge(rs2, b + 1)
                v.wait_ge(hx_ok, b + 1)
                v.scalar_tensor_tensor(out=acc[:, b % 2, :], in0=acc[:, b % 2, :], scalar=rst[:, 1, b:b + 1],
                                       in1=ln2r, op0=ALU.mult, op1=ALU.mult).then_inc(hn2, 1)

            att(0)
            att(1)
            for b in range(B + 3):
                if b < B:
                    gate_y(b)
                    low(b, hn[:, b % 2, :], y_hi, y_lo)
                if b + 2 < B:
                    att(b + 2)
                if 2 <= b < B + 2:
                    norm2(b - 2)
                if 1 <= b <= B:
                    add_h(b - 1)
                if b >= 3:
                    low(b - 3, bank[4][:, :], h2_hi, h2_lo)

            def hidden(n, m, par, hf):
                dst = hid[:, HB * hf:HB * (hf + 1), bass.ds(m * P, P)]
                v.wait_ge(sg_ok, n + 1)
                v.tensor_tensor(dst, blocks(hn[:, par, :]), blocks(bank[4 * par + 2 * hf + 1][:, :]), ALU.mult) \
                    .then_inc(hid_ok, 1)

            def ring_low(j, par):
                v.wait_ge(w_hi, 3 * j + (LOOP_CHUNK + par + 1))
                v.tensor_tensor(ringS[:, par, 1, :], raw[:, par, :], ringS[:, par, 0, :].bitcast(F32),
                                ALU.subtract).then_inc(ring_lo, 1)

            with v.Fori(0, NM // 2) as j:
                hidden(4 * j, 2 * j, 0, 0)
                hidden(4 * j + 1, 2 * j + 1, 1, 0)
                hidden(4 * j + 2, 2 * j, 0, 1)
                ring_low(j, 0)
                hidden(4 * j + 3, 2 * j + 1, 1, 1)
                ring_low(j, 1)

            def split_hid(t, par):
                v.wait_ge(hid_hi, t + 1)
                v.tensor_tensor(hidS[:, par, 1, :], big[:, bass.ds(t * (NM * P), NM * P)],
                                hidS[:, par, 0, :].bitcast(F32), ALU.subtract).then_inc(hid_lo, 1)

            def moments(i, t, u):
                v.wait_ge(ln_u[i], t + 1)
                v.bn_stats(stats[:, i, :], u).then_inc(ln_st[i], 1)
                v.wait_ge(ln_st[i], t + 1)
                v.bn_aggr(mv[:, i, :], stats[:, i, :]).then_inc(ln_mv[i], 1)

            def normed(i, t, u):
                v.wait_ge(ln_rs[i], t + 1)
                v.tensor_scalar(u, u, mv[:, i, 0:1], lrs[:, i:i + 1], ALU.subtract, ALU.mult).then_inc(ln_out[i], 1)

            def route(t):
                v.wait_ge(route_ps, t + 1)
                v.tensor_tensor(lg[:, 0, :], bank[7][:, 0:E], eb[:, :], ALU.add).then_inc(lg_step, 1)
                v.wait_ge(lg_step, 5 * t + 1)
                v.tensor_reduce(gm[:, 0:1], lg[:, 0, :], AX.X, ALU.max).then_inc(lg_step, 1)
                v.wait_ge(lg_step, 5 * t + 2)
                v.scalar_tensor_tensor(out=lg[:, 1, :], in0=lg[:, 0, :], scalar=gm[:, 0:1], in1=codes[:, :],
                                       op0=ALU.is_equal, op1=ALU.mult).then_inc(lg_step, 1)
                v.wait_ge(lg_step, 5 * t + 3)
                v.tensor_reduce(gm[:, 1:2], lg[:, 1, :], AX.X, ALU.max).then_inc(lg_step, 1)
                v.wait_ge(lg_step, 5 * t + 4)
                v.tensor_scalar(lg[:, 2, :], lg[:, 1, :], gm[:, 1:2], None, ALU.is_equal).then_inc(lg_step, 1)
                v.wait_ge(lg_step, 5 * t + 5)
                v.tensor_tensor(zm[:, 0:E * RANK].rearrange("p (e r) -> p e r", e=E),
                                bank[7][:, E:E + E * RANK].rearrange("p (e r) -> p e r", e=E),
                                lg[:, 2, :].unsqueeze(2).broadcast_to([P, E, RANK]), ALU.mult).then_inc(zm_ok, 1)

            def tail(t, par, a=True, f=True, g=True, split=True):
                if a:
                    v.wait_ge(down_ps, t)
                    v.tensor_tensor(u1, bank[1 - par][:, :], rows[:, bass.ds(t - 1, 1), :]
                                    .rearrange("p a n -> p (a n)"), ALU.add).then_inc(ln_u[0], 1)
                    moments(0, t - 1, u1)
                if g:
                    v.wait_ge(ffn_ps, t - 2)
                    if stored_wait[0]:
                        v.wait_ge(stored, 16 * (t - 3))
                    stored_wait[0] = True
                    v.tensor_tensor(u3, bank[6][:, :], u2[:, 1 - par, :], ALU.add).then_inc(ln_u[2], 1)
                    moments(2, t - 3, u3)
                if a:
                    normed(0, t - 1, u1)
                if g:
                    normed(2, t - 3, u3)
                if split:
                    split_hid(t + 1, 1 - par)
                if f:
                    v.wait_ge(x2_ok, t - 1)
                    v.tensor_copy(x2S[:, 0, :], x2T).then_inc(x2_hi, 1)
                    v.wait_ge(x2_hi, t - 1)
                    v.tensor_tensor(x2S[:, 1, :], x2T, x2S[:, 0, :].bitcast(F32), ALU.subtract).then_inc(x2_lo, 1)
                if a:
                    v.wait_ge(sc_ps, t)
                    v.tensor_reduce(sm[:, 0:1], bank[4][:, 0:P], AX.X, ALU.max, negate=True).then_inc(mx_ok, 1)
                if f:
                    route(t - 2)
                if a:
                    v.wait_ge(ex_ok, t)
                    v.reciprocal(sm[:, 2:3], sm[:, 1:2]).then_inc(rinv_ok, 1)
                    v.wait_ge(rinv_ok, t)
                    v.wait_ge(pv_ps, t)
                    v.scalar_tensor_tensor(out=u2[:, 1 - par, :], in0=bank[5][:, :], scalar=sm[:, 2:3], in1=u1,
                                           op0=ALU.mult, op1=ALU.add).then_inc(ln_u[1], 1)
                    moments(1, t - 1, u2[:, 1 - par, :])
                    normed(1, t - 1, u2[:, 1 - par, :])

            stored_wait = [False]
            v.wait_ge(zm_clear, 1)
            split_hid(0, 0)
            tail(0, 0, a=False, f=False, g=False)
            tail(1, 1, f=False, g=False)
            tail(2, 0, g=False)
            tail(3, 1)
            tail(4, 0)
            with v.Fori(2, B // 2 - 1) as j:
                tail(2 * j + 1, 1)
                tail(2 * j + 2, 0)
            tail(B - 1, 1, split=False)
            tail(B, 0, split=False)
            tail(B + 1, 1, a=False, split=False)
            tail(B + 2, 0, a=False, f=False, split=False)


def kernel(**inputs):
    import numpy as np
    from concourse import bacc
    from concourse.bass_utils import run_bass_kernel_spmd

    get = {k.replace("L0_", ""): np.asarray(v) for k, v in inputs.items()}

    def stationary(wT):
        return wT.reshape(DC, P, -1, P).transpose(2, 1, 0, 3).reshape(-1, P, D)

    w_inT = get["attn_w_in"].T
    inner = H * P
    dt_block = np.zeros((D, P), w_inT.dtype)
    dt_block[:, 0:H] = w_inT[:, 2 * inner + 2 * P:]
    in_blocks = stationary(np.concatenate([dt_block, w_inT[:, inner:2 * inner + 2 * P], w_inT[:, 0:inner],
                                           np.zeros((D, P), w_inT.dtype)], axis=1))
    gate, up = (stationary(get[k].T) for k in ("attn_gate_w", "attn_up_w"))

    def pairs(blocks):
        return blocks.reshape(-1, 2, P, D).transpose(0, 2, 1, 3).reshape(-1, P, CH)

    w_in = pairs(in_blocks)
    w_gu = np.concatenate([gate, up], axis=2)
    w_out, w_down, w_base = (pairs(get[k].T.reshape(-1, P, D)) for k in ("attn_w_out", "attn_down_w", "ffn_W_up"))
    ring = np.concatenate([w_gu, w_base])
    loop = [c for j in range(NM // 2) for c in (ring[2 * j + 2], ring[2 * j + 3], w_down[j])]
    wstream = np.concatenate([w_in, w_out, ring[0:2], np.stack(loop)])

    gate_lora = np.concatenate([get["ffn_gate_w"], get["ffn_lora_A"].reshape(E * RANK, D)]).T
    ctx = get["ctx_4096"]
    ins = {
        "x": get["x"], "ctx": ctx,
        "ctxT": ctx.transpose(0, 2, 1).reshape(B, DC, P, L).transpose(0, 2, 1, 3).reshape(B, P, D),
        "wstream": wstream,
        "conv_w": get["attn_conv_w"].reshape(N_CONV, P, 4).transpose(1, 0, 2),
        "conv_b": get["attn_conv_b"].reshape(N_CONV, P).T,
        "a_log": get["attn_A_log"].reshape(H, 1), "d_skip": get["attn_D"],
        "dt_bias": get["attn_dt_bias"].reshape(H, 1), "ln1_w": get["attn_ln1_w"], "ln2_w": get["attn_ln2_w"],
        "gate_lora": gate_lora.reshape(DC, P, -1).transpose(1, 0, 2), "expert_bias": get["ffn_expert_bias"],
        "lora_b": get["ffn_lora_B"].transpose(0, 2, 1).reshape(E * RANK, D),
    }
    nc = bacc.Bacc("TRN2", target_bir_lowering=False, num_devices=1)
    arrays, args = {}, []
    for name, a in ins.items():
        arrays[name] = np.ascontiguousarray(a)
        args.append(nc.dram_tensor(name, a.shape, F32, kind="ExternalInput").ap())
    args.append(nc.dram_tensor("out", (B, L, D), F32, kind="ExternalOutput").ap())
    build(nc, *args)
    r = run_bass_kernel_spmd(nc, [arrays], core_ids=[0])
    return r.results[0]["out"]
```

```python
from contextlib import ExitStack

import concourse.bass as bass
from concourse import mybir

F32 = mybir.dt.float32
F32R = mybir.dt.float32r
BF16 = mybir.dt.bfloat16
ALU = mybir.AluOpType
ACT = mybir.ActivationFunctionType
AX = mybir.AxisListType
LN_EXP = "natural_log_exp_and_others"

P = 128
D = 512
DC = D // P
B = 8
L = 128
TOK = B * L
HALF = TOK // 2
HB = B // 2
H = 4
INTER = 1792
NM = INTER // P
E = 4
RANK = 8
EPS = 1e-5
FUTURE = 1e30

CH = 1024
N_IN = 11
N_CONV = 6
IN_CHUNKS = (N_IN + 1) // 2
OUT_CHUNK = IN_CHUNKS
GU_CHUNK = OUT_CHUNK + 2
LOOP_CHUNK = GU_CHUNK + 2
N_CHUNKS = LOOP_CHUNK + 3 * (NM // 2)
RAW = 3

SEGS = ((0, 6), (6, 8), (8, 11), (11, 14))
PIECES = ((0, 2), (2, 6), (6, 14))

IN_ORDER = ((0, 0), (1, 0), (0, 1), (1, 1)) + tuple((m, hf) for m in range(2, N_IN) for hf in range(2))


N_CONST = 11


def raw_slot(n):
    return (n - LOOP_CHUNK) % RAW


def build(nc, x, ctx, ctxT, wstream, conv_w, conv_b, a_log, d_skip, dt_bias, ln1_w, ln2_w,
          gate_lora, expert_bias, lora_b, out):
    es = ExitStack()
    with es:
        def sb(name, shape, dt=F32):
            return es.enter_context(nc.sbuf_tensor(name, shape, dt))

        def sem(name):
            return es.enter_context(nc.semaphore(name))

        cols = sb("cols", [P, 8192], F32R)
        colsT = cols[:, :].rearrange("p (s c t) -> p s c t", s=2, c=DC)
        hidS = cols[:, 0:4 * NM * P].rearrange("p (b s n) -> p b s n", b=2, s=2)
        x2S = cols[:, 4 * NM * P:8192].rearrange("p (s n) -> p s n", s=2)
        wdS_t = sb("wdS", [P, 2 * NM * D], F32R)
        wdS = wdS_t[:, :].rearrange("p (s n) -> p s n", s=2)
        ringS_t = sb("ringS", [P, 2 * 2 * CH], F32R)
        ringS = ringS_t[:, :].rearrange("p (b s n) -> p b s n", b=2, s=2)
        rows = sb("rows", [P, B, D])
        big = sb("big", [P, NM * TOK])
        raw = sb("raw", [P, RAW, CH])
        tmp = sb("tmp", [P, 7 * D])
        szT = big[:, 0:4096].rearrange("p (h t) -> p h t", h=H)
        lb = big[0:3 * E * RANK, 0:D]
        cT = big[:, 4096:8192].rearrange("p (h t) -> p h t", h=H)
        xT = big[:, 8192:9216]
        bT = big[:, 9216:10240]
        dI = big[:, 10240:10752].rearrange("p (h q) -> p h q", h=H)
        dec = big[:, 10752:11776].rearrange("p (b h q) -> p b h q", b=2, h=H)
        negcs = big[0:H, 11776:12800]
        spare = big[:, 12800:13312].bitcast(BF16)
        sq_out = spare[:, 0:D]
        future = spare[:, D:2 * D].rearrange("p (h q) -> p h q", h=H)
        ln1r = big[:, 13312:13824]
        ln2r = big[:, 13824:14336]
        hid = big[:, :].rearrange("p (t n) -> p t n", t=B)
        hn = tmp[:, 0:1024].rearrange("p (b n) -> p b n", b=2)
        acc = tmp[:, 1024:2048].rearrange("p (b n) -> p b n", b=2)
        dt_row = tmp[0:H, 2048:3072]
        sel = tmp[0:H, 3072:3584].rearrange("p (h q) -> p h q", h=H)
        u1 = tmp[:, 0:512]
        u2 = tmp[:, 512:1536].rearrange("p (b n) -> p b n", b=2)
        u3 = tmp[:, 1536:2048]
        qT = tmp[:, 2048:2560]
        x2T = tmp[:, 2560:3072]
        ex = tmp[:, 3072:3200]
        exT = tmp[:, 3200:3328]
        zm = tmp[:, 3328:3456]
        stats = tmp[:, 3456:3474].rearrange("p (k s) -> p k s", k=3)
        lg = tmp[:, 3488:3488 + 3 * E].rearrange("p (k e) -> p k e", k=3)
        xb = sb("xb", [P, 2, P + 2 * H])
        ident = sb("ident", [P, P])
        identb = sb("identb", [P, P], BF16)
        ones = sb("ones", [H, P])
        small = sb("small", [P, 23])
        epsc = small[:, 0:1]
        onec = small[:, 1:2]
        cw = sb("cw", [P, N_CONV, 4])
        cb = sb("cb", [P, N_CONV])
        dsk = small[:, 5:5 + H]
        dtb = small[0:H, 2:3]
        alog = small[0:H, 3:4]
        expa = small[0:H, 4:5]
        ga = sb("ga", [P, DC, E + E * RANK])
        zmT = sb("zmT", [3 * E * RANK, P], F32R)
        lbS = sb("lbS", [3 * E * RANK, D], F32R)
        eb = sb("eb", [P, E])
        codes = sb("codes", [P, E])
        ssq = sb("ssq", [P, 2, B])
        rst = sb("rst", [P, 2, B])
        mv = small[:, 17:23].rearrange("p (k s) -> p k s", k=3)
        lrs = small[:, 9:12]
        sm = small[:, 12:15]
        gm = small[:, 15:17]

        bank = [es.enter_context(nc.psum_tensor(f"bank{i}", [P, D], F32)) for i in range(8)]

        x_in = [sem(f"x_in{t}") for t in range(B)]
        const_in = sem("const_in")
        ln1_in = sem("ln1_in")
        raw_in = [sem(f"raw_in{i}") for i in range(RAW)]
        ctx_in = [sem(f"ctx_in{i}") for i in range(2)]
        stored = sem("stored")
        pool_setup = sem("pool_setup")
        zm_clear = sem("zm_clear")
        vec_setup = sem("vec_setup")
        expa_ok = sem("expa_ok")
        w_hi = sem("w_hi")
        w_lo = sem("w_lo")
        ring_lo = sem("ring_lo")
        sq1, lr1, rs1, hn1 = sem("sq1"), sem("lr1"), sem("rs1"), sem("hn1")
        hT_ps, hT_hi, hT_lo = sem("hT_ps"), sem("hT_hi"), sem("hT_lo")
        ip_done, ip_used, z_done = sem("ip_done"), sem("ip_used"), sem("z_done")
        sp_step, sp_exp, sp_ln = sem("sp_step"), sem("sp_exp"), sem("sp_ln")
        dt_ok, a_ok, cs_ok = sem("dt_ok"), sem("a_ok"), sem("cs_ok")
        cv_init, cv_tap, cv_done = sem("cv_init"), sem("cv_tap"), sem("cv_done")
        s1_done, xb_ok, dec_exp = sem("s1_done"), sem("xb_ok"), sem("dec_exp")
        att_ok, attd_ok, y_ps, y_gated = sem("att_ok"), sem("attd_ok"), sem("y_ps"), sem("y_gated")
        y_hi, y_lo = sem("y_hi"), sem("y_lo")
        op_done, h_ok, hx_ok = sem("op_done"), sem("h_ok"), sem("hx_ok")
        sq2, lr2, rs2, hn2 = sem("sq2"), sem("lr2"), sem("rs2"), sem("hn2")
        h2_ps, h2_hi, h2_lo = sem("h2_ps"), sem("h2_hi"), sem("h2_lo")
        gu_done, sg_ok, hid_ok = sem("gu_done"), sem("sg_ok"), sem("hid_ok")
        first_hi, first_lo = sem("first_hi"), sem("first_lo")
        lb_ok = sem("lb_ok")
        hid_hi, hid_lo, down_ps = sem("hid_hi"), sem("hid_lo"), sem("down_ps")
        ln_u, ln_st, ln_mv, ln_log, ln_rs, ln_out = (
            [sem(f"ln{i}_{what}") for i in (1, 2, 3)] for what in ("u", "st", "mv", "log", "rs", "out"))
        q_ps, q_ok, sc_ps, mx_ok, ex_ok = sem("q_ps"), sem("q_ok"), sem("sc_ps"), sem("mx_ok"), sem("ex_ok")
        rinv_ok, exT_ps, exT_ok, pv_ps = sem("rinv_ok"), sem("exT_ps"), sem("exT_ok"), sem("pv_ps")
        x2_ps, x2_ok, x2_hi, x2_lo = sem("x2_ps"), sem("x2_ok"), sem("x2_hi"), sem("x2_lo")
        route_ps, lg_step, z_step, zm_ok = sem("route_ps"), sem("lg_step"), sem("z_step"), sem("zm_ok")
        zmT_ps, zmT_ok, ffn_ps = sem("zmT_ps"), sem("zmT_ok"), sem("ffn_ps")

        block = es.enter_context(nc.Block())

        def tok(b):
            return bass.ts(b, L)

        def half(hf):
            return bass.ts(hf, HALF)

        def blocks(ap):
            return ap.rearrange("p (c q) -> p c q", c=DC)

        def context(t):
            return (big[:, bass.ds(t * (NM * P), D)], big[:, bass.ds(t * (NM * P) + D, D)])


        @block.sync
        def _(sp):
            def load_chunk(n):
                sp.dma_start(raw[:, raw_slot(n), :], wstream[n]).then_inc(raw_in[raw_slot(n)], 16)

            for t in range(2):
                sp.dma_start(rows[:, t, :], x[t]).then_inc(x_in[t], 16)
            sp.dma_start(ln1r, ln1_w.partition_broadcast(P)).then_inc(ln1_in, 16)
            load_chunk(0)
            for t in range(2, HB):
                sp.dma_start(rows[:, t, :], x[t]).then_inc(x_in[t], 16)
            for dst, src in ((alog[:, :], a_log), (dtb[:, :], dt_bias), (cw[:, :, :], conv_w),
                             (cb[:, :], conv_b), (dsk[:, :], d_skip.partition_broadcast(P)),
                             (ln2r, ln2_w.partition_broadcast(P)), (ga[:, :, :], gate_lora),
                             *((lb[bass.ts(i, E * RANK), :], lora_b) for i in range(3)), (eb[:, :], expert_bias.partition_broadcast(P))):
                sp.dma_start(dst, src).then_inc(const_in, 16)
            for t in range(HB, B):
                sp.dma_start(rows[:, t, :], x[t]).then_inc(x_in[t], 16)
            load_chunk(1)
            load_chunk(2)
            for n in range(RAW, LOOP_CHUNK):
                sp.wait_ge(w_lo, n - RAW + 1)
                load_chunk(n)
            for i in range(RAW):
                sp.wait_ge(w_lo, LOOP_CHUNK + i - RAW + 1)
                load_chunk(LOOP_CHUNK + i)
            with sp.Fori(1, NM // 2) as j:
                chunks = [sp.snap(3 * j + (LOOP_CHUNK + i)) for i in range(RAW)]
                for i in range(RAW):
                    if i == 0:
                        sp.wait_ge(w_lo, j + LOOP_CHUNK)
                    else:
                        sp.wait_ge(ring_lo, 2 * j + (i - 2))
                    sp.dma_start(raw[:, i, :], wstream[bass.ds(chunks[i], 1)]
                                 .rearrange("a p n -> (a p) n")).then_inc(raw_in[i], 16)
            for t in range(B):
                sp.wait_ge(hid_lo if t else first_lo, t or len(PIECES))
                if t >= 2:
                    sp.wait_ge(ctx_in[t % 2], 32 * (t // 2))
                keyT, key = context(t)
                sp.dma_start(keyT, ctxT[t]).then_inc(ctx_in[t % 2], 16)
                sp.dma_start(key, ctx[t]).then_inc(ctx_in[t % 2], 16)
            sp.wait_ge(stored, 16 * B)

        @block.gpsimd
        def _(pool):
            pool.memset(ident[:, :], 0.0).then_inc(pool_setup, 1)
            pool.memset(sel, 1.0).then_inc(pool_setup, 1)
            pool.wait_ge(pool_setup, 2)
            pool.affine_select(out=ident[:, :], in_=ident[:, :], compare_op=ALU.not_equal, fill=1.0,
                               base=0, pattern=[[-1, P]], channel_multiplier=1).then_inc(pool_setup, 1)
            pool.affine_select(out=sel, in_=sel, compare_op=ALU.is_equal, fill=0.0,
                               base=0, pattern=[[-1, H], [0, P]], channel_multiplier=1).then_inc(pool_setup, 1)
            pool.memset(future, 0.0).then_inc(pool_setup, 1)
            pool.wait_ge(pool_setup, 5)
            pool.tensor_copy(identb[:, :], ident[:, :]).then_inc(pool_setup, 1)
            pool.affine_select(out=future, in_=future, compare_op=ALU.is_ge, fill=FUTURE, base=0,
                               pattern=[[0, H], [1, L]], channel_multiplier=-1).then_inc(pool_setup, 1)
            for e in range(E):
                mm = pool.memset(codes[:, e:e + 1], float(E - e))
            mm.then_inc(pool_setup, 1)

            def lo_part(n, dst, hi):
                pool.wait_ge(w_hi, n + 1)
                pool.tensor_tensor(dst, raw[:, raw_slot(n), :], hi.bitcast(F32), ALU.subtract).then_inc(w_lo, 1)

            for n in range(IN_CHUNKS):
                lo_part(n, ringS[:, n % 2, 1, :], ringS[:, n % 2, 0, :])
            for i in range(2):
                lo_part(OUT_CHUNK + i, wdS[:, 1, bass.ts(i, CH)], wdS[:, 0, bass.ts(i, CH)])

            def skip(b):
                d = dec[:, b % 2, :, :]
                if b == 0:
                    pool.wait_ge(vec_setup, 2)
                pool.wait_ge(att_ok, H * (b + 1))
                pool.tensor_tensor(d, d, dI, ALU.add).then_inc(attd_ok, 1)

            def residual(b):
                pool.wait_ge(h_ok, b + 1)
                pool.tensor_tensor(rows[:, b, :], rows[:, b, :], acc[:, b % 2, :], ALU.add).then_inc(hx_ok, 1)

            skip(0)
            skip(1)
            for b in range(B + 1):
                if b >= 1:
                    residual(b - 1)
                if b + 2 < B:
                    skip(b + 2)
                if b == 2:
                    for i in range(2):
                        lo_part(GU_CHUNK + i, ringS[:, i, 1, :], ringS[:, i, 0, :])
            pool.memset(zm, 0.0).then_inc(zm_clear, 1)
            with pool.Fori(0, NM // 2) as j:
                pool.wait_ge(w_hi, 3 * j + (LOOP_CHUNK + 1))
                pool.tensor_tensor(wdS_t[:, bass.ds(j * CH + NM * D, CH)], raw[:, 0, :],
                                   wdS_t[:, bass.ds(j * CH, CH)].bitcast(F32), ALU.subtract).then_inc(w_lo, 1)

        IPB = 3
        N_DVE_IP = 2 + 2 * N_CONV

        def conv_product(i):
            return IN_ORDER.index((1 + i // 2, i % 2))

        def three_pass(pe, ps, a_hi, a_lo, b_hi, b_lo, first, last):
            pe.matmul(ps, a_hi, b_lo, start=first, stop=False)
            pe.matmul(ps, a_hi, b_hi, start=False, stop=False)
            return pe.matmul(ps, a_lo, b_hi, start=False, stop=last)

        @block.tensor
        def _(pe):
            def turn_h(t):
                pe.wait_ge(hn1, t + 1)
                if t >= 2:
                    pe.wait_ge(hT_lo, t - 1)
                for c in range(DC):
                    mm = pe.transpose(bank[t % 2][:, bass.ts(c, P)], hn[:, t % 2, bass.ts(c, P)], ident[:, :])
                mm.then_inc(hT_ps, 1)

            def in_proj(n):
                m, hf = IN_ORDER[n]
                pe.wait_ge(w_lo, m // 2 + 1)
                pe.wait_ge(hT_lo, HB * (hf + 1))
                before = n - IPB
                if 0 <= before < N_DVE_IP:
                    pe.wait_ge(ip_used, before + 1)
                elif before >= N_DVE_IP:
                    pe.wait_ge(z_done, before - N_DVE_IP + 1)
                w = ringS[:, (m // 2) % 2, :, bass.ts(m % 2, D)]
                for c in range(DC):
                    mm = three_pass(pe, bank[2 + n % IPB][:, :], w[:, 0, bass.ts(c, P)], w[:, 1, bass.ts(c, P)],
                                    colsT[:, 0, c, half(hf)], colsT[:, 1, c, half(hf)], c == 0, c == DC - 1)
                mm.then_inc(ip_done, 1)

            def scores_of(b):
                pe.wait_ge(cs_ok, b + 1)
                pe.wait_ge(cv_done, 2 * N_CONV - 1 + b // HB)
                if b >= 2:
                    pe.wait_ge(dec_exp, H * (b - 1))
                if b >= 1:
                    pe.wait_ge(xb_ok, b)
                    pe.wait_ge(att_ok, H * b)
                pe.matmul(bank[b % 2][:, :], identb[:, :], future, start=True, stop=False)
                for h in range(H):
                    pe.matmul(bank[b % 2][:, bass.ts(h, L)], sel[:, h, :], negcs[:, tok(b)],
                              start=False, stop=(h == H - 1))
                pe.transpose(bank[5][:, 0:P], xT[:, tok(b)], ident[:, :])
                pe.transpose(bank[5][:, P:P + H], negcs[:, tok(b)], ident[0:H, 0:H])
                pe.transpose(bank[5][:, P + H:P + 2 * H], dt_row[:, tok(b)], ident[0:H, 0:H])
                pe.matmul(bank[6][:, :], bT[:, tok(b)], cT[:, :, tok(b)], start=True, stop=True).then_inc(s1_done, 1)

            def y_of(b):
                pe.wait_ge(attd_ok, b + 1)
                pe.wait_ge(xb_ok, b + 1)
                if b >= 1:
                    pe.wait_ge(y_gated, b)
                pe.matmul(bank[7][:, :], xb[:, b % 2, 0:P], dec[:, b % 2, :, :], start=True, stop=True) \
                    .then_inc(y_ps, 1)

            def out_proj(b):
                if b == 0:
                    pe.wait_ge(w_lo, OUT_CHUNK + 2)
                    pe.wait_ge(z_done, 2 * H)
                pe.wait_ge(y_lo, b + 1)
                if b >= 2:
                    pe.wait_ge(h_ok, b - 1)
                for c in range(DC):
                    mm = three_pass(pe, bank[2 + b % 2][:, :], colsT[:, 0, c, tok(b)], colsT[:, 1, c, tok(b)],
                                    wdS[:, 0, bass.ts(c, D)], wdS[:, 1, bass.ts(c, D)], c == 0, c == DC - 1)
                mm.then_inc(op_done, 1)

            def turn_h2(b, bk):
                pe.wait_ge(hn2, b + 1)
                if b >= 1:
                    pe.wait_ge(h2_lo, b if bk == 4 else B - 2)
                for c in range(DC):
                    mm = pe.transpose(bank[bk][:, bass.ts(c, P)], acc[:, b % 2, bass.ts(c, P)], ident[:, :])
                mm.then_inc(h2_ps, 1)

            def gate_up(par, hf):
                for g in range(2):
                    for c in range(DC):
                        col = g * D + c * P
                        mm = three_pass(pe, bank[4 * par + 2 * hf + g][:, :],
                                        ringS[:, par, 0, col:col + P], ringS[:, par, 1, col:col + P],
                                        colsT[:, 0, c, half(hf)], colsT[:, 1, c, half(hf)], c == 0, c == DC - 1)
                mm.then_inc(gu_done, 1)

            pe.wait_ge(pool_setup, 8)
            for t in range(HB):
                turn_h(t)
            in_proj(0)
            turn_h(HB)
            turn_h(HB + 1)
            in_proj(1)
            turn_h(HB + 2)
            turn_h(HB + 3)
            scores_after = {N_DVE_IP + 1: 0, N_DVE_IP + 3: 1, N_DVE_IP + 6: 2}
            for n in range(2, 2 * N_IN):
                in_proj(n)
                if n in scores_after:
                    scores_of(scores_after[n])
            for b in range(B + 1):
                if b < B:
                    y_of(b)
                if b >= 3:
                    turn_h2(b - 3, 4)
                if b >= 1:
                    out_proj(b - 1)
                if 1 <= b < B - 2:
                    scores_of(b + 2)
            pe.wait_ge(w_lo, LOOP_CHUNK)
            pe.wait_ge(h2_lo, B - 2)
            gate_up(0, 0)
            turn_h2(B - 2, 6)
            turn_h2(B - 1, 7)
            gate_up(1, 0)
            pe.wait_ge(h2_lo, B)
            gate_up(0, 1)
            gate_up(1, 1)
            with pe.Fori(1, NM // 2) as j:
                for hf in range(2):
                    for par in range(2):
                        if hf == 0:
                            pe.wait_ge(ring_lo, 2 * j + (par - 1))
                        pe.wait_ge(hid_ok, 4 * j + (2 * hf + par - 3))
                        gate_up(par, hf)

            def down(t, par, seg, first_use):
                k0, k1 = SEGS[seg]
                if k0 == 0 and not (isinstance(t, int) and t == 0):
                    pe.wait_ge(hid_lo, t)
                    if not first_use:
                        pe.wait_ge(ln_u[0], t - 1)
                for k in range(k0, k1):
                    if isinstance(t, int) and t == 0:
                        for i, (p0, _) in enumerate(PIECES):
                            if p0 == k:
                                pe.wait_ge(first_lo, i + 1)
                    mm = three_pass(pe, bank[par][:, :], hidS[:, par, 0, bass.ts(k, P)],
                                    hidS[:, par, 1, bass.ts(k, P)], wdS[:, 0, bass.ts(k, D)],
                                    wdS[:, 1, bass.ts(k, D)], k == 0, k == NM - 1)
                if k1 == NM:
                    mm.then_inc(down_ps, 1)

            def turn_x1(t):
                pe.wait_ge(ln_out[0], t + 1)
                for c in range(DC):
                    mm = pe.transpose(bank[2][:, bass.ts(c, P)], u1[:, bass.ts(c, P)], ident[:, :])
                mm.then_inc(q_ps, 1)

            def attend(t, par):
                pe.wait_ge(q_ok, t + 1)
                pe.wait_ge(ctx_in[par], 16 * (t + 2 - par))
                keyT, _ = context(t)
                for c in range(DC):
                    mm = pe.matmul(bank[4][:, 0:P], qT[:, bass.ts(c, P)], blocks(keyT)[:, c, :],
                                   start=(c == 0), stop=(c == DC - 1))
                mm.then_inc(sc_ps, 1)

            def turn_ex(t):
                pe.wait_ge(ex_ok, t + 1)
                pe.transpose(bank[4][:, P:2 * P], ex, ident[:, :]).then_inc(exT_ps, 1)

            def mix(t):
                pe.wait_ge(exT_ok, t + 1)
                _, key = context(t)
                pe.matmul(bank[5][:, :], exT, key, start=True, stop=True).then_inc(pv_ps, 1)

            def turn_x2(t, par):
                pe.wait_ge(ln_out[1], t + 1)
                for c in range(DC):
                    mm = pe.transpose(bank[3][:, bass.ts(c, P)], u2[:, par, bass.ts(c, P)], ident[:, :])
                mm.then_inc(x2_ps, 1)

            def route_and_base(t, first_use):
                pe.wait_ge(x2_ok, t + 1)
                for c in range(DC):
                    mm = pe.matmul(bank[7][:, 0:E + E * RANK], x2T[:, bass.ts(c, P)], ga[:, c, :],
                                   start=(c == 0), stop=(c == DC - 1))
                mm.then_inc(route_ps, 1)
                pe.wait_ge(x2_lo, t + 1)
                if first_use:
                    pe.wait_ge(ring_lo, NM)
                else:
                    pe.wait_ge(ln_u[2], t)
                for c in range(DC):
                    three_pass(pe, bank[6][:, :], x2S[:, 0, bass.ts(c, P)], x2S[:, 1, bass.ts(c, P)],
                               ringS[:, c // 2, 0, bass.ts(c % 2, D)], ringS[:, c // 2, 1, bass.ts(c % 2, D)],
                               c == 0, False)

            def turn_z(t):
                pe.wait_ge(zm_ok, t + 1)
                pe.transpose(bank[7][:, P:2 * P], zm, ident[:, :]).then_inc(zmT_ps, 1)

            def lora(t):
                pe.wait_ge(zmT_ok, t + 1)
                pe.matmul(bank[6][:, :], zmT[:, :], lbS[:, :], start=False, stop=True).then_inc(ffn_ps, 1)

            def tail(t, par, d=True, a=True, f=True, first_d=False, first_f=False):
                if d:
                    down(t, par, 0, first_d)
                if a:
                    turn_x1(t - 1)
                if f:
                    turn_x2(t - 2, par)
                if d:
                    down(t, par, 1, first_d)
                if a:
                    attend(t - 1, 1 - par)
                if f:
                    route_and_base(t - 2, first_f)
                if a:
                    turn_ex(t - 1)
                if d:
                    down(t, par, 2, first_d)
                if f:
                    turn_z(t - 2)
                if a:
                    mix(t - 1)
                if d:
                    down(t, par, 3, first_d)
                if f:
                    lora(t - 2)

            pe.wait_ge(w_lo, LOOP_CHUNK + NM // 2)
            pe.wait_ge(lb_ok, 2)
            tail(0, 0, a=False, f=False, first_d=True)
            tail(1, 1, f=False, first_d=True)
            tail(2, 0, first_f=True)
            with pe.Fori(1, B // 2 - 1) as j:
                tail(2 * j + 1, 1)
                tail(2 * j + 2, 0)
            tail(B - 1, 1)
            tail(B, 0, d=False)
            tail(B + 1, 1, d=False, a=False)

        @block.scalar
        def _(act):
            def hi_part(n, dst):
                landed = sum(raw_slot(i) == raw_slot(n) for i in range(n + 1))
                act.wait_ge(raw_in[raw_slot(n)], 16 * landed)
                act.activation(dst, raw[:, raw_slot(n), :], ACT.Copy).then_inc(w_hi, 1)

            def ring_hi(n):
                if n >= 2:
                    act.wait_ge(ip_done, 4 * (n - 1))
                hi_part(n, ringS[:, n % 2, 0, :])

            def squares(i, t, src, squared):
                act.activation(sq_out, src, ACT.Square, accum_out=ssq[:, i, t:t + 1]).then_inc(squared, 1)

            def rms(i, t0, t1, squared, logged, done):
                r = rst[:, i, t0:t1]
                act.wait_ge(squared, t1)
                act.activation(r, ssq[:, i, t0:t1], ACT.Ln, bias=epsc[:, :], scale=1.0 / D).then_inc(logged, t1 - t0)
                act.wait_ge(logged, t1)
                act.activation(r, r, ACT.Exp, scale=-0.5).then_inc(done, t1 - t0)

            def norm1(t0, t1):
                for t in range(t0, t1):
                    act.wait_ge(x_in[t], 16)
                    if t:
                        act.wait_ge(sq1, t)
                    squares(0, t, rows[:, t, :], sq1)
                if t0 == 0:
                    act.wait_ge(vec_setup, 1)
                rms(0, t0, t1, sq1, lr1, rs1)

            def hi_of_hT(t):
                act.wait_ge(hT_ps, t + 1)
                act.activation(colsT[:, 0, :, tok(t)], blocks(bank[t % 2][:, :]), ACT.Copy).then_inc(hT_hi, 1)

            def softplus(hf):
                v = negcs[:, half(hf)]
                act.wait_ge(sp_step, 3 * (hf + 1))
                act.activation(v, v, ACT.Exp).then_inc(sp_exp, 1)
                act.wait_ge(sp_exp, hf + 1)
                act.activation(v, v, ACT.Ln, bias=onec[0:H, :]).then_inc(sp_ln, 1)

            def conv_last_tap(i):
                m, n = i // 2, conv_product(i)
                act.wait_ge(ip_done, n + 1)
                if i >= 2:
                    act.wait_ge(cv_done, i - 1)
                act.activation(acc[:, i % 2, :], bank[2 + n % IPB][:, :], ACT.Identity,
                               bias=cb[:, m:m + 1], scale=cw[:, m, 3:4]).then_inc(cv_init, 1)

            def conv_silu(i):
                m, hf = i // 2, i % 2
                act.wait_ge(cv_tap, 3 * (i + 1))
                dst = xT[:, half(hf)] if m == 0 else bT[:, half(hf)] if m == 1 else cT[:, m - 2, half(hf)]
                act.activation(dst, acc[:, i % 2, :], ACT.Silu).then_inc(cv_done, 1)

            def z_silu(i):
                n = N_DVE_IP + i
                act.wait_ge(ip_done, n + 1)
                if i == 0:
                    act.wait_ge(lb_ok, 2)
                act.activation(szT[:, i // 2, half(i % 2)], bank[2 + n % IPB][:, :], ACT.Silu).then_inc(z_done, 1)

            def decay(b):
                act.wait_ge(s1_done, b + 1)
                if b >= 2:
                    act.wait_ge(y_ps, b - 1)
                act.activation(xb[:, b % 2, :], bank[5][:, 0:P + 2 * H], ACT.Copy).then_inc(xb_ok, 1)
                act.wait_ge(xb_ok, b + 1)
                for h in range(H):
                    act.activation(dec[:, b % 2, h, :], bank[b % 2][:, bass.ts(h, L)], ACT.Exp,
                                   bias=xb[:, b % 2, P + h:P + h + 1], scale=-1.0).then_inc(dec_exp, 1)

            def hi_of_y(b):
                act.wait_ge(y_gated, b + 1)
                act.activation(colsT[:, 0, :, tok(b)], blocks(hn[:, b % 2, :]), ACT.Copy).then_inc(y_hi, 1)

            def norm2(b):
                act.wait_ge(h_ok, b + 1)
                squares(1, b, acc[:, b % 2, :], sq2)
                rms(1, b, b + 1, sq2, lr2, rs2)

            def hi_of_h2(b, bk):
                act.wait_ge(h2_ps, b + 1)
                act.activation(colsT[:, 0, :, tok(b)], blocks(bank[bk][:, :]), ACT.Copy).then_inc(h2_hi, 1)

            act.preload_act_table_set(LN_EXP)
            norm1(0, 2)
            hi_of_hT(0)
            norm1(2, HB)
            hi_part(0, ringS[:, 0, 0, :])
            for t in range(1, HB):
                hi_of_hT(t)
            norm1(HB, HB + 2)
            hi_of_hT(HB)
            norm1(HB + 2, B)
            for t in range(HB + 1, B):
                hi_of_hT(t)
            conv_last_tap(0)
            act.wait_ge(const_in, 16 * N_CONST)
            act.activation(expa[:, :], alog[:, :], ACT.Exp).then_inc(expa_ok, 1)
            softplus(0)
            ring_hi(1)
            softplus(1)
            for i in range(1, 2 * N_CONV):
                conv_last_tap(i)
                conv_silu(i - 1)
                if i % 4 == 1:
                    ring_hi(2 + i // 4)
            conv_silu(2 * N_CONV - 1)
            z_silu(0)
            z_silu(1)
            ring_hi(IN_CHUNKS - 1)
            act.preload_act_table_set(LN_EXP)
            decay(0)
            decay(1)
            for i in range(2, 2 * H):
                z_silu(i)
                if i in (4, 5):
                    hi_part(OUT_CHUNK + i - 4, wdS[:, 0, bass.ts(i - 4, CH)])
            act.preload_act_table_set(LN_EXP)
            for b in range(B + 1):
                if b < B:
                    hi_of_y(b)
                if b >= 3:
                    hi_of_h2(b - 3, 4)
                if b >= 1:
                    norm2(b - 1)
                if b + 2 < B:
                    decay(b + 2)
                if b == 1:
                    for i in range(2):
                        act.wait_ge(ip_done, 2 * N_IN)
                        hi_part(GU_CHUNK + i, ringS[:, i, 0, :])
            hi_of_h2(B - 2, 6)
            hi_of_h2(B - 1, 7)

            def sg(v, par, hf, first_use):
                act.wait_ge(gu_done, v + 1)
                if not first_use:
                    act.wait_ge(hid_ok, v - 1)
                act.activation(hn[:, par, :], bank[4 * par + 2 * hf][:, :], ACT.Silu).then_inc(sg_ok, 1)

            landed = [sum(raw_slot(n) == i for n in range(LOOP_CHUNK)) for i in range(RAW)]

            def loop_hi(j, i, dst):
                act.wait_ge(raw_in[i], 16 * j + 16 * (landed[i] + 1))
                act.activation(dst, raw[:, i, :], ACT.Copy).then_inc(w_hi, 1)

            def pair(j, first_use):
                sg(4 * j, 0, 0, first_use)
                sg(4 * j + 1, 1, 0, first_use)
                loop_hi(j, 0, wdS_t[:, bass.ds(j * CH, CH)])
                sg(4 * j + 2, 0, 1, False)
                loop_hi(j, 1, ringS[:, 0, 0, :])
                sg(4 * j + 3, 1, 1, False)

            pair(0, True)
            loop_hi(0, 2, ringS[:, 1, 0, :])
            with act.Fori(1, NM // 2 - 1) as j:
                pair(j, False)
                loop_hi(j, 2, ringS[:, 1, 0, :])
            pair(NM // 2 - 1, False)
            act.wait_ge(hid_ok, 2 * NM - 2)
            for k0, k1 in PIECES:
                act.activation(hidS[:, 0, 0, k0 * P:k1 * P], big[:, k0 * P:k1 * P], ACT.Copy).then_inc(first_hi, 1)
            loop_hi(NM // 2 - 1, 2, ringS[:, 1, 0, :])

            def split_hid(t, par, first_use=False):
                if not first_use:
                    act.wait_ge(down_ps, t - 1)
                act.activation(hidS[:, par, 0, :], big[:, bass.ds(t * (NM * P), NM * P)], ACT.Copy) \
                    .then_inc(hid_hi, 1)

            def rstd(i, t):
                act.wait_ge(ln_mv[i], t + 1)
                act.activation(lrs[:, i:i + 1], mv[:, i, 1:2], ACT.Ln, bias=epsc[:, :]).then_inc(ln_log[i], 1)
                act.wait_ge(ln_log[i], t + 1)
                act.activation(lrs[:, i:i + 1], lrs[:, i:i + 1], ACT.Exp, scale=-0.5).then_inc(ln_rs[i], 1)

            def store(t):
                act.wait_ge(ln_out[2], t + 1)
                act.dma_start(out[bass.ds(t, 1)].rearrange("a p n -> (a p) n"), u3).then_inc(stored, 16)

            def tail(t, par, a=True, f=True, g=True, split=True, first_split=False):
                if a:
                    rstd(0, t - 1)
                if g:
                    rstd(2, t - 3)
                if split:
                    split_hid(t + 1, 1 - par, first_split)
                if a:
                    act.wait_ge(q_ps, t)
                    act.activation(qT, bank[2][:, :], ACT.Copy).then_inc(q_ok, 1)
                if f:
                    act.wait_ge(x2_ps, t - 1)
                    act.activation(x2T, bank[3][:, :], ACT.Copy).then_inc(x2_ok, 1)
                if g:
                    store(t - 3)
                if a:
                    act.wait_ge(mx_ok, t)
                    act.activation(ex, bank[4][:, 0:P], ACT.Exp, bias=sm[:, 0:1], accum_out=sm[:, 1:2]) \
                        .then_inc(ex_ok, 1)
                    act.wait_ge(exT_ps, t)
                    act.activation(exT, bank[4][:, P:2 * P], ACT.Copy).then_inc(exT_ok, 1)
                if f:
                    act.wait_ge(zmT_ps, t - 1)
                    act.activation(zmT[:, :], bank[7][0:3 * E * RANK, P:2 * P], ACT.Copy).then_inc(zmT_ok, 1)
                if a:
                    rstd(1, t - 1)

            act.preload_act_table_set(LN_EXP)
            act.wait_ge(hid_ok, 2 * NM)
            tail(0, 0, a=False, f=False, g=False, first_split=True)
            tail(1, 1, f=False, g=False)
            tail(2, 0, g=False)
            with act.Fori(1, B // 2 - 1) as j:
                tail(2 * j + 1, 1)
                tail(2 * j + 2, 0)
            tail(B - 1, 1, split=False)
            tail(B, 0, split=False)
            tail(B + 1, 1, a=False, split=False)
            tail(B + 2, 0, a=False, f=False, split=False)

        @block.vector
        def _(v):
            v.memset(epsc[:, :], EPS)
            v.memset(ones[:, :], 1.0)
            v.memset(onec[:, :], 1.0).then_inc(vec_setup, 1)

            def norm1(t):
                v.wait_ge(rs1, t + 1)
                if t == 0:
                    v.wait_ge(ln1_in, 16)
                if t >= 2:
                    v.wait_ge(hT_ps, t - 1)
                v.scalar_tensor_tensor(out=hn[:, t % 2, :], in0=rows[:, t, :], scalar=rst[:, 0, t:t + 1],
                                       in1=ln1r, op0=ALU.mult, op1=ALU.mult).then_inc(hn1, 1)

            def low(t, src, hi_ready, done):
                v.wait_ge(hi_ready, t + 1)
                v.tensor_tensor(colsT[:, 1, :, tok(t)], blocks(src), colsT[:, 0, :, tok(t)].bitcast(F32),
                                ALU.subtract).then_inc(done, 1)

            def low1(t):
                low(t, bank[t % 2][:, :], hT_hi, hT_lo)

            for t0 in (0, HB):
                norm1(t0)
                for t in range(t0 + 1, t0 + HB):
                    norm1(t)
                    low1(t - 1)
                low1(t0 + HB - 1)

            def softplus_in(hf):
                n = IN_ORDER.index((0, hf))
                dst, n_ps = negcs[:, half(hf)], bank[2 + n % IPB][0:H, :]
                v.wait_ge(ip_done, n + 1)
                if hf == 0:
                    v.wait_ge(const_in, 16 * N_CONST)
                v.tensor_scalar(dt_row[:, half(hf)], n_ps, dtb[:, 0:1], 0.0, ALU.add, ALU.max).then_inc(sp_step, 1)
                v.tensor_scalar(dst, n_ps, dtb[:, 0:1], None, ALU.add).then_inc(sp_step, 1)
                v.wait_ge(sp_step, 3 * hf + 2)
                v.scalar_tensor_tensor(out=dst, in0=dst, scalar=-1.0, in1=dst, op0=ALU.mult, op1=ALU.min) \
                    .then_inc(sp_step, 1)
                v.sem_inc(ip_used, 1)

            def time_steps(hf):
                h_ = half(hf)
                v.wait_ge(sp_ln, hf + 1)
                v.tensor_tensor(dt_row[:, h_], dt_row[:, h_], negcs[:, h_], ALU.add).then_inc(dt_ok, 1)
                v.wait_ge(dt_ok, hf + 1)
                v.wait_ge(expa_ok, 1)
                v.tensor_scalar(negcs[:, h_], dt_row[:, h_], expa[:, 0:1], None, ALU.mult).then_inc(a_ok, 1)
                v.wait_ge(a_ok, hf + 1)
                for b in range(HB * hf, HB * (hf + 1)):
                    v.tensor_tensor_scan(negcs[:, tok(b)], ones[:, :], negcs[:, tok(b)], 0.0,
                                         ALU.mult, ALU.add).then_inc(cs_ok, 1)

            def conv_taps(i):
                m = i // 2
                src = bank[2 + conv_product(i) % IPB][:, :].rearrange("p (b q) -> p b q", b=HB)
                dst = acc[:, i % 2, :].rearrange("p (b q) -> p b q", b=HB)
                v.wait_ge(cv_init, i + 1)
                for s in range(1, 4):
                    if s > 1:
                        v.wait_ge(cv_tap, 3 * i + s - 1)
                    v.scalar_tensor_tensor(out=dst[:, :, s:L], in0=src[:, :, 0:L - s],
                                           scalar=cw[:, m, 3 - s:4 - s], in1=dst[:, :, s:L],
                                           op0=ALU.mult, op1=ALU.add).then_inc(cv_tap, 1)
                v.wait_ge(cv_tap, 3 * i + 3)
                v.sem_inc(ip_used, 1)

            softplus_in(0)
            conv_taps(0)
            softplus_in(1)
            conv_taps(1)
            time_steps(0)
            for h in range(H):
                if h == 0:
                    v.wait_ge(pool_setup, 8)
                mm = v.tensor_scalar(dI[:, h, :], ident[:, :], dsk[:, h:h + 1], None, ALU.mult)
            mm.then_inc(vec_setup, 1)
            v.tensor_copy(lbS[:, :], lb[:, :]).then_inc(lb_ok, 1)
            v.wait_ge(lb_ok, 1)
            last = slice(2 * E * RANK, 3 * E * RANK)
            v.tensor_tensor(lbS[last, :], lb[last, :], lbS[last, :].bitcast(F32), ALU.subtract).then_inc(lb_ok, 1)
            for i in range(2, 2 * N_CONV):
                conv_taps(i)
                if i == 3:
                    time_steps(1)

            def att(b):
                v.wait_ge(dec_exp, H * (b + 1))
                for h in range(H):
                    v.scalar_tensor_tensor(out=dec[:, b % 2, h, :], in0=bank[6][:, bass.ts(h, L)],
                                           scalar=xb[:, b % 2, P + H + h:P + H + h + 1],
                                           in1=dec[:, b % 2, h, :], op0=ALU.mult, op1=ALU.mult).then_inc(att_ok, 1)

            def gate_y(b):
                v.wait_ge(y_ps, b + 1)
                if b == 0:
                    v.wait_ge(z_done, 2 * H)
                v.tensor_tensor(blocks(hn[:, b % 2, :]), blocks(bank[7][:, :]), szT[:, :, tok(b)], ALU.mult) \
                    .then_inc(y_gated, 1)

            def add_h(b):
                v.wait_ge(op_done, b + 1)
                if b >= 2:
                    v.wait_ge(h2_ps, b - 1)
                v.tensor_tensor(acc[:, b % 2, :], bank[2 + b % 2][:, :], rows[:, b, :], ALU.add).then_inc(h_ok, 1)

            def norm2(b):
                v.wait_ge(rs2, b + 1)
                v.wait_ge(hx_ok, b + 1)
                v.scalar_tensor_tensor(out=acc[:, b % 2, :], in0=acc[:, b % 2, :], scalar=rst[:, 1, b:b + 1],
                                       in1=ln2r, op0=ALU.mult, op1=ALU.mult).then_inc(hn2, 1)

            att(0)
            att(1)
            for b in range(B + 1):
                if b < B:
                    gate_y(b)
                    low(b, hn[:, b % 2, :], y_hi, y_lo)
                if b >= 3:
                    low(b - 3, bank[4][:, :], h2_hi, h2_lo)
                if b >= 2:
                    norm2(b - 2)
                if b >= 1:
                    add_h(b - 1)
                if b + 2 < B:
                    att(b + 2)
            norm2(B - 1)
            low(B - 2, bank[6][:, :], h2_hi, h2_lo)
            low(B - 1, bank[7][:, :], h2_hi, h2_lo)

            def hidden(n, m, par, hf):
                dst = hid[:, HB * hf:HB * (hf + 1), bass.ds(m * P, P)]
                v.wait_ge(sg_ok, n + 1)
                v.tensor_tensor(dst, blocks(hn[:, par, :]), blocks(bank[4 * par + 2 * hf + 1][:, :]), ALU.mult) \
                    .then_inc(hid_ok, 1)

            def ring_low(j, par):
                v.wait_ge(w_hi, 3 * j + (LOOP_CHUNK + par + 2))
                v.tensor_tensor(ringS[:, par, 1, :], raw[:, par + 1, :], ringS[:, par, 0, :].bitcast(F32),
                                ALU.subtract).then_inc(ring_lo, 1)

            def pair(j):
                hidden(4 * j, 2 * j, 0, 0)
                hidden(4 * j + 1, 2 * j + 1, 1, 0)
                hidden(4 * j + 2, 2 * j, 0, 1)
                ring_low(j, 0)
                hidden(4 * j + 3, 2 * j + 1, 1, 1)

            with v.Fori(0, NM // 2 - 1) as j:
                pair(j)
                ring_low(j, 1)
            pair(NM // 2 - 1)
            for i, (k0, k1) in enumerate(PIECES):
                v.wait_ge(first_hi, i + 1)
                v.tensor_tensor(hidS[:, 0, 1, k0 * P:k1 * P], big[:, k0 * P:k1 * P],
                                hidS[:, 0, 0, k0 * P:k1 * P].bitcast(F32), ALU.subtract).then_inc(first_lo, 1)
            ring_low(NM // 2 - 1, 1)

            def split_hid(t, par):
                v.wait_ge(hid_hi, t)
                v.tensor_tensor(hidS[:, par, 1, :], big[:, bass.ds(t * (NM * P), NM * P)],
                                hidS[:, par, 0, :].bitcast(F32), ALU.subtract).then_inc(hid_lo, 1)

            def moments(i, t, u):
                v.wait_ge(ln_u[i], t + 1)
                v.bn_stats(stats[:, i, :], u).then_inc(ln_st[i], 1)
                v.wait_ge(ln_st[i], t + 1)
                v.bn_aggr(mv[:, i, :], stats[:, i, :]).then_inc(ln_mv[i], 1)

            def normed(i, t, u):
                v.wait_ge(ln_rs[i], t + 1)
                v.tensor_scalar(u, u, mv[:, i, 0:1], lrs[:, i:i + 1], ALU.subtract, ALU.mult).then_inc(ln_out[i], 1)

            def route(t):
                v.wait_ge(route_ps, t + 1)
                v.tensor_tensor(lg[:, 0, :], bank[7][:, 0:E], eb[:, :], ALU.add).then_inc(lg_step, 1)
                v.wait_ge(lg_step, 5 * t + 1)
                v.tensor_reduce(gm[:, 0:1], lg[:, 0, :], AX.X, ALU.max).then_inc(lg_step, 1)
                v.wait_ge(lg_step, 5 * t + 2)
                v.scalar_tensor_tensor(out=lg[:, 1, :], in0=lg[:, 0, :], scalar=gm[:, 0:1], in1=codes[:, :],
                                       op0=ALU.is_equal, op1=ALU.mult).then_inc(lg_step, 1)
                v.wait_ge(lg_step, 5 * t + 3)
                v.tensor_reduce(gm[:, 1:2], lg[:, 1, :], AX.X, ALU.max).then_inc(lg_step, 1)
                v.wait_ge(lg_step, 5 * t + 4)
                v.tensor_scalar(lg[:, 2, :], lg[:, 1, :], gm[:, 1:2], None, ALU.is_equal).then_inc(lg_step, 1)
                v.wait_ge(lg_step, 5 * t + 5)
                er = E * RANK
                z = zm[:, 3 * er:4 * er]
                v.tensor_tensor(z.rearrange("p (e r) -> p e r", e=E),
                                bank[7][:, E:E + er].rearrange("p (e r) -> p e r", e=E),
                                lg[:, 2, :].unsqueeze(2).broadcast_to([P, E, RANK]), ALU.mult).then_inc(z_step, 1)
                v.wait_ge(z_step, 2 * t + 1)
                v.tensor_copy(zm[:, 0:4 * er].rearrange("p (a b r) -> p a b r", a=2, b=2)[:, :, 0, :].bitcast(F32R),
                              z.unsqueeze(1).broadcast_to([P, 2, er])).then_inc(z_step, 1)
                v.wait_ge(z_step, 2 * t + 2)
                v.tensor_tensor(zm[:, er:2 * er].bitcast(F32R), z, zm[:, 0:er], ALU.subtract).then_inc(zm_ok, 1)

            def tail(t, par, a=True, f=True, g=True, split=True):
                if a:
                    v.wait_ge(down_ps, t)
                    v.tensor_tensor(u1, bank[1 - par][:, :], rows[:, bass.ds(t - 1, 1), :]
                                    .rearrange("p a n -> p (a n)"), ALU.add).then_inc(ln_u[0], 1)
                    moments(0, t - 1, u1)
                if g:
                    v.wait_ge(ffn_ps, t - 2)
                    if stored_wait[0]:
                        v.wait_ge(stored, 16 * (t - 3))
                    stored_wait[0] = True
                    v.tensor_tensor(u3, bank[6][:, :], u2[:, 1 - par, :], ALU.add).then_inc(ln_u[2], 1)
                    moments(2, t - 3, u3)
                if a:
                    normed(0, t - 1, u1)
                if g:
                    normed(2, t - 3, u3)
                if split:
                    split_hid(t + 1, 1 - par)
                if f:
                    v.wait_ge(x2_ok, t - 1)
                    v.tensor_copy(x2S[:, 0, :], x2T).then_inc(x2_hi, 1)
                    v.wait_ge(x2_hi, t - 1)
                    v.tensor_tensor(x2S[:, 1, :], x2T, x2S[:, 0, :].bitcast(F32), ALU.subtract).then_inc(x2_lo, 1)
                if a:
                    v.wait_ge(sc_ps, t)
                    v.tensor_reduce(sm[:, 0:1], bank[4][:, 0:P], AX.X, ALU.max, negate=True).then_inc(mx_ok, 1)
                if f:
                    route(t - 2)
                if a:
                    v.wait_ge(ex_ok, t)
                    v.reciprocal(sm[:, 2:3], sm[:, 1:2]).then_inc(rinv_ok, 1)
                    v.wait_ge(rinv_ok, t)
                    v.wait_ge(pv_ps, t)
                    v.scalar_tensor_tensor(out=u2[:, 1 - par, :], in0=bank[5][:, :], scalar=sm[:, 2:3], in1=u1,
                                           op0=ALU.mult, op1=ALU.add).then_inc(ln_u[1], 1)
                    moments(1, t - 1, u2[:, 1 - par, :])
                    normed(1, t - 1, u2[:, 1 - par, :])

            stored_wait = [False]
            v.wait_ge(zm_clear, 1)
            tail(0, 0, a=False, f=False, g=False)
            tail(1, 1, f=False, g=False)
            tail(2, 0, g=False)
            tail(3, 1)
            tail(4, 0)
            with v.Fori(2, B // 2 - 1) as j:
                tail(2 * j + 1, 1)
                tail(2 * j + 2, 0)
            tail(B - 1, 1, split=False)
            tail(B, 0, split=False)
            tail(B + 1, 1, a=False, split=False)
            tail(B + 2, 0, a=False, f=False, split=False)


def kernel(**inputs):
    import numpy as np
    from concourse import bacc
    from concourse.bass_utils import run_bass_kernel_spmd

    get = {k.replace("L0_", ""): np.asarray(v) for k, v in inputs.items()}

    def stationary(wT):
        return wT.reshape(DC, P, -1, P).transpose(2, 1, 0, 3).reshape(-1, P, D)

    w_inT = get["attn_w_in"].T
    inner = H * P
    dt_block = np.zeros((D, P), w_inT.dtype)
    dt_block[:, 0:H] = w_inT[:, 2 * inner + 2 * P:]
    in_blocks = stationary(np.concatenate([dt_block, w_inT[:, inner:2 * inner + 2 * P], w_inT[:, 0:inner],
                                           np.zeros((D, P), w_inT.dtype)], axis=1))
    gate, up = (stationary(get[k].T) for k in ("attn_gate_w", "attn_up_w"))

    def pairs(blocks):
        return blocks.reshape(-1, 2, P, D).transpose(0, 2, 1, 3).reshape(-1, P, CH)

    w_in = pairs(in_blocks)
    w_gu = np.concatenate([gate, up], axis=2)
    w_out, w_down, w_base = (pairs(get[k].T.reshape(-1, P, D)) for k in ("attn_w_out", "attn_down_w", "ffn_W_up"))
    ring = np.concatenate([w_gu, w_base])
    loop = [c for j in range(NM // 2) for c in (w_down[j], ring[2 * j + 2], ring[2 * j + 3])]
    wstream = np.concatenate([w_in, w_out, ring[0:2], np.stack(loop)])

    gate_lora = np.concatenate([get["ffn_gate_w"], get["ffn_lora_A"].reshape(E * RANK, D)]).T
    ctx = get["ctx_4096"]
    ins = {
        "x": get["x"], "ctx": ctx,
        "ctxT": ctx.transpose(0, 2, 1).reshape(B, DC, P, L).transpose(0, 2, 1, 3).reshape(B, P, D),
        "wstream": wstream,
        "conv_w": get["attn_conv_w"].reshape(N_CONV, P, 4).transpose(1, 0, 2),
        "conv_b": get["attn_conv_b"].reshape(N_CONV, P).T,
        "a_log": get["attn_A_log"].reshape(H, 1), "d_skip": get["attn_D"],
        "dt_bias": get["attn_dt_bias"].reshape(H, 1), "ln1_w": get["attn_ln1_w"], "ln2_w": get["attn_ln2_w"],
        "gate_lora": gate_lora.reshape(DC, P, -1).transpose(1, 0, 2), "expert_bias": get["ffn_expert_bias"],
        "lora_b": get["ffn_lora_B"].transpose(0, 2, 1).reshape(E * RANK, D),
    }
    nc = bacc.Bacc("TRN2", target_bir_lowering=False, num_devices=1)
    arrays, args = {}, []
    for name, a in ins.items():
        arrays[name] = np.ascontiguousarray(a)
        args.append(nc.dram_tensor(name, a.shape, F32, kind="ExternalInput").ap())
    args.append(nc.dram_tensor("out", (B, L, D), F32, kind="ExternalOutput").ap())
    build(nc, *args)
    r = run_bass_kernel_spmd(nc, [arrays], core_ids=[0])
    return r.results[0]["out"]
```

```python
from contextlib import ExitStack

import concourse.bass as bass
from concourse import mybir

F32 = mybir.dt.float32
F32R = mybir.dt.float32r
BF16 = mybir.dt.bfloat16
ALU = mybir.AluOpType
ACT = mybir.ActivationFunctionType
AX = mybir.AxisListType
LN_EXP = "natural_log_exp_and_others"

P = 128
D = 512
DC = D // P
B = 8
L = 128
TOK = B * L
HALF = TOK // 2
HB = B // 2
H = 4
INTER = 1792
NM = INTER // P
E = 4
RANK = 8
EPS = 1e-5
FUTURE = 1e30

CH = 1024
N_IN = 11
N_CONV = 6
IN_CHUNKS = (N_IN + 1) // 2
OUT_CHUNK = IN_CHUNKS
GU_CHUNK = OUT_CHUNK + 2
LOOP_CHUNK = GU_CHUNK + 2
RAW = 3

SEGS = ((0, 8), (8, 10), (10, 12), (12, 14))
END_SEGS = ((0, 8), (8, 9), (9, 10), (10, 11), (11, 14))

IN_ORDER = ((0, 0), (1, 0), (0, 1), (1, 1)) + tuple((m, hf) for m in range(2, N_IN) for hf in range(2))
N_CONST = 11


def raw_slot(n):
    return (n - LOOP_CHUNK) % RAW


def build(nc, x, ctx, ctxT, wstream, conv_w, conv_b, a_log, d_skip, dt_bias, ln1_w, ln2_w,
          gate_lora, expert_bias, lora_b, out):
    es = ExitStack()
    with es:
        def sb(name, shape, dt=F32):
            return es.enter_context(nc.sbuf_tensor(name, shape, dt))

        def sem(name):
            return es.enter_context(nc.semaphore(name))

        cols_t = sb("cols", [P, 2 * 2 * DC * HALF], F32R)
        cols = cols_t[:, :].rearrange("p (b s n) -> p b s n", b=2, s=2)
        colsT = cols_t[:, :].rearrange("p (b s c t) -> p b s c t", b=2, s=2, c=DC)
        hidS = cols[:, :, :, 0:NM * P]
        x2S = cols[:, :, :, NM * P:NM * P + 2 * P]
        wdS_t = sb("wdS", [P, 2 * NM * D], F32R)
        wdS = wdS_t[:, :].rearrange("p (s n) -> p s n", s=2)
        ringS_t = sb("ringS", [P, 2 * 2 * CH], F32R)
        ringS = ringS_t[:, :].rearrange("p (b s n) -> p b s n", b=2, s=2)
        rows = sb("rows", [P, B, D])
        big = sb("big", [P, NM * TOK])
        raw = sb("raw", [P, RAW, CH])
        tmp = sb("tmp", [P, 7 * D])
        szT = big[:, 0:4096].rearrange("p (h t) -> p h t", h=H)
        lb = big[0:3 * E * RANK, 0:D]
        cT = big[:, 4096:8192].rearrange("p (h t) -> p h t", h=H)
        xT = big[:, 8192:9216]
        bT = big[:, 9216:10240]
        dI = big[:, 10240:10752].rearrange("p (h q) -> p h q", h=H)
        dec = big[:, 10752:11776].rearrange("p (b h q) -> p b h q", b=2, h=H)
        negcs = big[0:H, 11776:12800]
        spare = big[:, 12800:13312].bitcast(BF16)
        sq_out = spare[:, 0:D]
        future = spare[:, D:2 * D].rearrange("p (h q) -> p h q", h=H)
        ln1r = big[:, 13312:13824]
        ln2r = big[:, 13824:14336]
        hid = big[:, :].rearrange("p (t n) -> p t n", t=B)
        hn = tmp[:, 0:1024].rearrange("p (b n) -> p b n", b=2)
        acc = tmp[:, 1024:2048].rearrange("p (b n) -> p b n", b=2)
        dt_row = tmp[0:H, 2048:3072]
        sel = tmp[0:H, 3072:3584].rearrange("p (h q) -> p h q", h=H)
        u1 = tmp[:, 0:512]
        u2 = tmp[:, 512:1536].rearrange("p (b n) -> p b n", b=2)
        u3 = tmp[:, 1536:2048]
        qT = tmp[:, 2048:2560]
        u_last = qT
        x2T = tmp[:, 2560:3072]
        ex = tmp[:, 3072:3200]
        exT = tmp[:, 3200:3328]
        zm = tmp[:, 3328:3456]
        stats = tmp[:, 3456:3474].rearrange("p (k s) -> p k s", k=3)
        lg = tmp[:, 3488:3488 + 3 * E].rearrange("p (k e) -> p k e", k=3)
        idle = dec[:, 0, 0:2, :].bitcast(BF16)
        xb = sb("xb", [P, 2, P + 2 * H])
        ident = sb("ident", [P, P])
        identb = sb("identb", [P, P], BF16)
        ones = sb("ones", [H, P])
        small = sb("small", [P, 23])
        epsc = small[:, 0:1]
        onec = small[:, 1:2]
        cw = sb("cw", [P, N_CONV, 4])
        cb = sb("cb", [P, N_CONV])
        dsk = small[:, 5:5 + H]
        dtb = small[0:H, 2:3]
        alog = small[0:H, 3:4]
        expa = small[0:H, 4:5]
        ga = sb("ga", [P, DC, E + E * RANK])
        zmT = sb("zmT", [3 * E * RANK, P], F32R)
        lbS = sb("lbS", [3 * E * RANK, D], F32R)
        eb = sb("eb", [P, E])
        codes = sb("codes", [P, E])
        ssq = sb("ssq", [P, 2, B])
        rst = sb("rst", [P, 2, B])
        mv = small[:, 17:23].rearrange("p (k s) -> p k s", k=3)
        lrs = small[:, 9:12]
        sm = small[:, 12:15]
        gm = small[:, 15:17]

        bank = [es.enter_context(nc.psum_tensor(f"bank{i}", [P, D], F32)) for i in range(8)]

        x_in = [sem(f"x_in{t}") for t in range(B)]
        const_in = sem("const_in")
        ln1_in = sem("ln1_in")
        raw_in = [sem(f"raw_in{i}") for i in range(RAW)]
        ctx_in = [sem(f"ctx_in{i}") for i in range(2)]
        stored = sem("stored")
        pool_setup = sem("pool_setup")
        zm_clear = sem("zm_clear")
        vec_setup = sem("vec_setup")
        idle_ok = sem("idle_ok")
        expa_ok = sem("expa_ok")
        w_hi = sem("w_hi")
        w_lo = sem("w_lo")
        ring_lo = sem("ring_lo")
        sq1, lr1, rs1, hn1 = sem("sq1"), sem("lr1"), sem("rs1"), sem("hn1")
        hT_ps, hT_hi, hT_lo = sem("hT_ps"), sem("hT_hi"), sem("hT_lo")
        ip_done, ip_used, z_done = sem("ip_done"), sem("ip_used"), sem("z_done")
        sp_step, sp_exp, sp_ln = sem("sp_step"), sem("sp_exp"), sem("sp_ln")
        dt_ok, a_ok, cs_ok = sem("dt_ok"), sem("a_ok"), sem("cs_ok")
        cv_init, cv_tap, cv_done = sem("cv_init"), sem("cv_tap"), sem("cv_done")
        s1_done, xb_ok, dec_exp = sem("s1_done"), sem("xb_ok"), sem("dec_exp")
        att_ok, attd_ok, y_ps, y_gated = sem("att_ok"), sem("attd_ok"), sem("y_ps"), sem("y_gated")
        y_hi, y_lo = sem("y_hi"), sem("y_lo")
        op_done, h_ok, hx_ok = sem("op_done"), sem("h_ok"), sem("hx_ok")
        sq2, lr2, rs2, hn2 = sem("sq2"), sem("lr2"), sem("rs2"), sem("hn2")
        h2_ps, h2_hi, h2_lo = sem("h2_ps"), sem("h2_hi"), sem("h2_lo")
        gu_done, sg_ok, hid_ok = sem("gu_done"), sem("sg_ok"), sem("hid_ok")
        lb_ok = sem("lb_ok")
        hid_hi, hid_lo, down_ps = sem("hid_hi"), sem("hid_lo"), sem("down_ps")
        ln_u, ln_st, ln_mv, ln_log, ln_rs, ln_out = (
            [sem(f"ln{i}_{what}") for i in (1, 2, 3)] for what in ("u", "st", "mv", "log", "rs", "out"))
        q_ps, q_ok, sc_ps, mx_ok, ex_ok = sem("q_ps"), sem("q_ok"), sem("sc_ps"), sem("mx_ok"), sem("ex_ok")
        rinv_ok, exT_ps, exT_ok, pv_ps = sem("rinv_ok"), sem("exT_ps"), sem("exT_ok"), sem("pv_ps")
        x2_ps, x2_ok, x2_hi, x2_lo = sem("x2_ps"), sem("x2_ok"), sem("x2_hi"), sem("x2_lo")
        route_ps, lg_step, z_step, zm_ok = sem("route_ps"), sem("lg_step"), sem("z_step"), sem("zm_ok")
        zmT_ps, zmT_ok, ffn_ps = sem("zmT_ps"), sem("zmT_ok"), sem("ffn_ps")

        block = es.enter_context(nc.Block())

        def tok(b):
            return bass.ts(b, L)

        def token_cols(t, part):
            return colsT[:, t // HB, part, :, bass.ts(t % HB, P)]

        def half(hf):
            return bass.ts(hf, HALF)

        def blocks(ap):
            return ap.rearrange("p (c q) -> p c q", c=DC)

        def context(t):
            return (big[:, bass.ds(t * (NM * P), D)], big[:, bass.ds(t * (NM * P) + D, D)])


        @block.sync
        def _(sp):
            def load_chunk(n):
                sp.dma_start(raw[:, raw_slot(n), :], wstream[n]).then_inc(raw_in[raw_slot(n)], 16)

            for t in range(2):
                sp.dma_start(rows[:, t, :], x[t]).then_inc(x_in[t], 16)
            sp.dma_start(ln1r, ln1_w.partition_broadcast(P)).then_inc(ln1_in, 16)
            for t in range(2, HB):
                sp.dma_start(rows[:, t, :], x[t]).then_inc(x_in[t], 16)
            load_chunk(0)
            for dst, src in ((alog[:, :], a_log), (dtb[:, :], dt_bias), (cw[:, :, :], conv_w),
                             (cb[:, :], conv_b), (dsk[:, :], d_skip.partition_broadcast(P)),
                             (ln2r, ln2_w.partition_broadcast(P)), (ga[:, :, :], gate_lora),
                             *((lb[bass.ts(i, E * RANK), :], lora_b) for i in range(3)),
                             (eb[:, :], expert_bias.partition_broadcast(P))):
                sp.dma_start(dst, src).then_inc(const_in, 16)
            for t in range(HB, B):
                sp.dma_start(rows[:, t, :], x[t]).then_inc(x_in[t], 16)
            load_chunk(1)
            load_chunk(2)
            for n in range(RAW, LOOP_CHUNK):
                sp.wait_ge(w_lo, n - RAW + 1)
                load_chunk(n)
            for i in range(RAW):
                sp.wait_ge(w_lo, LOOP_CHUNK + i - RAW + 1)
                load_chunk(LOOP_CHUNK + i)
            with sp.Fori(1, NM // 2) as j:
                chunks = [sp.snap(3 * j + (LOOP_CHUNK + i)) for i in range(RAW)]
                for i in range(RAW):
                    if i == 0:
                        sp.wait_ge(w_lo, j + LOOP_CHUNK)
                    else:
                        sp.wait_ge(ring_lo, 2 * j + (i - 2))
                    sp.dma_start(raw[:, i, :], wstream[bass.ds(chunks[i], 1)]
                                 .rearrange("a p n -> (a p) n")).then_inc(raw_in[i], 16)
            for t in range(B):
                sp.wait_ge(hid_lo, t + 1)
                if t >= 2:
                    sp.wait_ge(ctx_in[t % 2], 32 * (t // 2))
                keyT, key = context(t)
                sp.dma_start(keyT, ctxT[t]).then_inc(ctx_in[t % 2], 16)
                sp.dma_start(key, ctx[t]).then_inc(ctx_in[t % 2], 16)
            sp.wait_ge(stored, 16 * B)

        @block.gpsimd
        def _(pool):
            pool.memset(ident[:, :], 0.0).then_inc(pool_setup, 1)
            pool.memset(sel, 1.0).then_inc(pool_setup, 1)
            pool.wait_ge(pool_setup, 2)
            pool.affine_select(out=ident[:, :], in_=ident[:, :], compare_op=ALU.not_equal, fill=1.0,
                               base=0, pattern=[[-1, P]], channel_multiplier=1).then_inc(pool_setup, 1)
            pool.affine_select(out=sel, in_=sel, compare_op=ALU.is_equal, fill=0.0,
                               base=0, pattern=[[-1, H], [0, P]], channel_multiplier=1).then_inc(pool_setup, 1)
            pool.memset(future, 0.0).then_inc(pool_setup, 1)
            pool.wait_ge(pool_setup, 5)
            pool.tensor_copy(identb[:, :], ident[:, :]).then_inc(pool_setup, 1)
            pool.affine_select(out=future, in_=future, compare_op=ALU.is_ge, fill=FUTURE, base=0,
                               pattern=[[0, H], [1, L]], channel_multiplier=-1).then_inc(pool_setup, 1)
            for e in range(E):
                mm = pool.memset(codes[:, e:e + 1], float(E - e))
            mm.then_inc(pool_setup, 1)

            def lo_part(n, dst, hi):
                pool.wait_ge(w_hi, n + 1)
                pool.tensor_tensor(dst, raw[:, raw_slot(n), :], hi.bitcast(F32), ALU.subtract).then_inc(w_lo, 1)

            for n in range(IN_CHUNKS):
                lo_part(n, ringS[:, n % 2, 1, :], ringS[:, n % 2, 0, :])
                if n == 0:
                    pool.wait_ge(const_in, 16 * N_CONST)
                    pool.tensor_copy(lbS[:, :], lb[:, :]).then_inc(lb_ok, 1)
                    pool.wait_ge(lb_ok, 1)
                    third = slice(2 * E * RANK, 3 * E * RANK)
                    pool.tensor_tensor(lbS[third, :], lb[third, :], lbS[third, :].bitcast(F32), ALU.subtract) \
                        .then_inc(lb_ok, 1)
                    pool.wait_ge(lb_ok, 2)

            def skip(b):
                d = dec[:, b % 2, :, :]
                if b == 0:
                    pool.wait_ge(vec_setup, 2)
                pool.wait_ge(att_ok, H * (b + 1))
                pool.tensor_tensor(d, d, dI, ALU.add).then_inc(attd_ok, 1)

            def residual(b):
                pool.wait_ge(h_ok, b + 1)
                pool.tensor_tensor(rows[:, b, :], rows[:, b, :], acc[:, b % 2, :], ALU.add).then_inc(hx_ok, 1)

            skip(0)
            skip(1)
            for i in range(2):
                lo_part(OUT_CHUNK + i, wdS[:, 1, bass.ts(i, CH)], wdS[:, 0, bass.ts(i, CH)])
            for b in range(B + 1):
                if b + 2 < B:
                    skip(b + 2)
                if b >= 1:
                    residual(b - 1)
                if b == 4:
                    for i in range(2):
                        lo_part(GU_CHUNK + i, ringS[:, i, 1, :], ringS[:, i, 0, :])
            pool.memset(zm, 0.0).then_inc(zm_clear, 1)
            with pool.Fori(0, NM // 2) as j:
                pool.wait_ge(w_hi, 3 * j + (LOOP_CHUNK + 1))
                pool.tensor_tensor(wdS_t[:, bass.ds(j * CH + NM * D, CH)], raw[:, 0, :],
                                   wdS_t[:, bass.ds(j * CH, CH)].bitcast(F32), ALU.subtract).then_inc(w_lo, 1)

        N_DVE_IP = 2 + 2 * N_CONV
        IN_BANK = [2 + n % 6 if n <= N_DVE_IP else (7, 2, 3, 4)[(n - N_DVE_IP - 1) % 4] for n in range(2 * N_IN)]

        def conv_product(i):
            return IN_ORDER.index((1 + i // 2, i % 2))

        def three_pass(pe, ps, a_hi, a_lo, b_hi, b_lo, first, last):
            pe.matmul(ps, a_hi, b_lo, start=first, stop=False)
            pe.matmul(ps, a_hi, b_hi, start=False, stop=False)
            return pe.matmul(ps, a_lo, b_hi, start=False, stop=last)

        @block.tensor
        def _(pe):
            def turn_h(t):
                pe.wait_ge(hn1, t + 1)
                if t >= 2:
                    pe.wait_ge(hT_lo, t - 1)
                for c in range(DC):
                    mm = pe.transpose(bank[t % 2][:, bass.ts(c, P)], hn[:, t % 2, bass.ts(c, P)], ident[:, :])
                mm.then_inc(hT_ps, 1)

            def in_proj(n, parts=1, part=0):
                m, hf = IN_ORDER[n]
                width = HALF // parts
                pe.wait_ge(w_lo, m // 2 + 1)
                pe.wait_ge(hT_lo, HB * hf + (part + 1) * HB // parts)
                for before in range(n - 1, -1, -1):
                    if IN_BANK[before] == IN_BANK[n]:
                        if before < N_DVE_IP:
                            pe.wait_ge(ip_used, before + 1)
                        else:
                            pe.wait_ge(z_done, before - N_DVE_IP + 1)
                        break
                w = ringS[:, (m // 2) % 2, :, bass.ts(m % 2, D)]
                q = bass.ts(part, width)
                for c in range(DC):
                    mm = three_pass(pe, bank[IN_BANK[n]][:, bass.ts(part, width)], w[:, 0, bass.ts(c, P)],
                                    w[:, 1, bass.ts(c, P)], colsT[:, hf, 0, c, q], colsT[:, hf, 1, c, q],
                                    c == 0, c == DC - 1)
                if part == parts - 1:
                    mm.then_inc(ip_done, 1)

            def scores_of(b):
                pe.wait_ge(cs_ok, b + 1)
                if b >= 2:
                    pe.wait_ge(dec_exp, H * (b - 1))
                pe.matmul(bank[b % 2][:, :], identb[:, :], future, start=True, stop=False)
                for h in range(H):
                    pe.matmul(bank[b % 2][:, bass.ts(h, L)], sel[:, h, :], negcs[:, tok(b)],
                              start=False, stop=(h == H - 1))
                pe.wait_ge(cv_done, 2 * N_CONV - 1 + b // HB)
                if b == 0:
                    pe.wait_ge(ip_used, N_DVE_IP)
                else:
                    pe.wait_ge(xb_ok, b)
                pe.transpose(bank[5][:, 0:P], xT[:, tok(b)], ident[:, :])
                pe.transpose(bank[5][:, P:P + H], negcs[:, tok(b)], ident[0:H, 0:H])
                pe.transpose(bank[5][:, P + H:P + 2 * H], dt_row[:, tok(b)], ident[0:H, 0:H])
                if b >= 1:
                    pe.wait_ge(att_ok, H * b)
                pe.matmul(bank[6][:, :], bT[:, tok(b)], cT[:, :, tok(b)], start=True, stop=True).then_inc(s1_done, 1)

            def y_of(b):
                pe.wait_ge(attd_ok, b + 1)
                pe.wait_ge(xb_ok, b + 1)
                if b >= 1:
                    pe.wait_ge(y_gated, b)
                else:
                    pe.wait_ge(z_done, 6)
                pe.matmul(bank[7][:, :], xb[:, b % 2, 0:P], dec[:, b % 2, :, :], start=True, stop=True) \
                    .then_inc(y_ps, 1)

            def out_proj(b):
                if b == 0:
                    pe.wait_ge(w_lo, OUT_CHUNK + 2)
                    pe.wait_ge(z_done, 2 * H)
                pe.wait_ge(y_lo, b + 1)
                if b >= 2:
                    pe.wait_ge(h_ok, b - 1)
                for c in range(DC):
                    mm = three_pass(pe, bank[2 + b % 2][:, :],
                                    token_cols(b, 0)[:, c, :], token_cols(b, 1)[:, c, :],
                                    wdS[:, 0, bass.ts(c, D)], wdS[:, 1, bass.ts(c, D)], c == 0, c == DC - 1)
                mm.then_inc(op_done, 1)

            def turn_h2(b, bk):
                pe.wait_ge(hn2, b + 1)
                if b >= 1:
                    pe.wait_ge(h2_lo, b if bk == 4 else B - 2)
                for c in range(DC):
                    mm = pe.transpose(bank[bk][:, bass.ts(c, P)], acc[:, b % 2, bass.ts(c, P)], ident[:, :])
                mm.then_inc(h2_ps, 1)

            def gate_up(par, hf, parts=(0, 1)):
                for g in parts:
                    for c in range(DC):
                        col = g * D + c * P
                        mm = three_pass(pe, bank[4 * par + 2 * hf + g][:, :],
                                        ringS[:, par, 0, col:col + P], ringS[:, par, 1, col:col + P],
                                        colsT[:, hf, 0, c, :], colsT[:, hf, 1, c, :], c == 0, c == DC - 1)
                if g == 1:
                    mm.then_inc(gu_done, 1)

            def keep_warm(count, bk, weights, values):
                for _ in range(count):
                    pe.matmul(bank[bk][:, :], weights, values, start=True, stop=True)

            zeros = (7, idle[:, 0, 0:P], idle)
            WARM = (4, 4, 2, 2, 2)
            pe.wait_ge(idle_ok, 1)
            keep_warm(12, *zeros)
            pe.wait_ge(pool_setup, 8)
            turn_h(0)
            turn_h(1)
            keep_warm(WARM[0], *zeros)
            turn_h(2)
            keep_warm(WARM[1], *zeros)
            in_proj(0, 2, 0)
            turn_h(3)
            in_proj(1, 2, 0)
            keep_warm(WARM[2], *zeros)
            in_proj(0, 2, 1)
            turn_h(4)
            in_proj(1, 2, 1)
            turn_h(5)
            keep_warm(WARM[3], *zeros)
            turn_h(6)
            in_proj(2, 2, 0)
            turn_h(7)
            in_proj(3, 2, 0)
            keep_warm(WARM[4], *zeros)
            in_proj(2, 2, 1)
            in_proj(3, 2, 1)
            scores_after = {N_DVE_IP + 3: 0, N_DVE_IP + 5: 1}
            for n in range(4, 2 * N_IN):
                in_proj(n)
                if n in scores_after:
                    scores_of(scores_after[n])
            for b in range(B + 1):
                if b < B:
                    y_of(b)
                if 3 <= b < B - 2:
                    scores_of(b + 2)
                if b == B - 1:
                    pe.wait_ge(w_lo, LOOP_CHUNK)
                    pe.wait_ge(h2_lo, HB)
                    gate_up(0, 0, (0,))
                if b == B:
                    gate_up(0, 0, (1,))
                if b >= 3:
                    turn_h2(b - 3, 4)
                if b >= 1:
                    out_proj(b - 1)
                if b < 3:
                    scores_of(b + 2)
            pe.wait_ge(h2_lo, B - 2)
            gate_up(1, 0, (0,))
            turn_h2(B - 2, 6)
            turn_h2(B - 1, 7)
            gate_up(1, 0, (1,))
            pe.wait_ge(h2_lo, B)
            gate_up(0, 1)
            gate_up(1, 1)
            with pe.Fori(1, NM // 2) as j:
                for hf in range(2):
                    for par in range(2):
                        if hf == 0:
                            pe.wait_ge(ring_lo, 2 * j + (par - 1))
                        pe.wait_ge(hid_ok, 4 * j + (2 * hf + par - 3))
                        gate_up(par, hf)

            def down(t, par, seg, first_use, segs=SEGS):
                k0, k1 = segs[seg]
                if k0 == 0:
                    pe.wait_ge(hid_lo, t + 1)
                    if not first_use:
                        pe.wait_ge(ln_u[0], t - 1)
                for k in range(k0, k1):
                    mm = three_pass(pe, bank[par][:, :], hidS[:, par, 0, bass.ts(k, P)],
                                    hidS[:, par, 1, bass.ts(k, P)], wdS[:, 0, bass.ts(k, D)],
                                    wdS[:, 1, bass.ts(k, D)], k == 0, k == NM - 1)
                if k1 == NM:
                    mm.then_inc(down_ps, 1)

            def turn_x1(t):
                pe.wait_ge(ln_out[0], t + 1)
                for c in range(DC):
                    mm = pe.transpose(bank[2][:, bass.ts(c, P)], u1[:, bass.ts(c, P)], ident[:, :])
                mm.then_inc(q_ps, 1)

            def attend(t, par):
                pe.wait_ge(q_ok, t + 1)
                pe.wait_ge(ctx_in[par], 16 * (t + 2 - par))
                keyT, _ = context(t)
                for c in range(DC):
                    mm = pe.matmul(bank[4][:, 0:P], qT[:, bass.ts(c, P)], blocks(keyT)[:, c, :],
                                   start=(c == 0), stop=(c == DC - 1))
                mm.then_inc(sc_ps, 1)

            def turn_ex(t):
                pe.wait_ge(ex_ok, t + 1)
                pe.transpose(bank[4][:, P:2 * P], ex, ident[:, :]).then_inc(exT_ps, 1)

            def mix(t):
                pe.wait_ge(exT_ok, t + 1)
                _, key = context(t)
                pe.matmul(bank[5][:, :], exT, key, start=True, stop=True).then_inc(pv_ps, 1)

            def turn_x2(t, par):
                pe.wait_ge(ln_out[1], t + 1)
                for c in range(DC):
                    mm = pe.transpose(bank[3][:, bass.ts(c, P)], u2[:, par, bass.ts(c, P)], ident[:, :])
                mm.then_inc(x2_ps, 1)

            def route(t, bk=7):
                pe.wait_ge(x2_ok, t + 1)
                for c in range(DC):
                    mm = pe.matmul(bank[bk][:, 0:E + E * RANK], x2T[:, bass.ts(c, P)], ga[:, c, :],
                                   start=(c == 0), stop=(c == DC - 1))
                mm.then_inc(route_ps, 1)

            def base(t, first_use=False, bk=6):
                pe.wait_ge(x2_lo, t + 1)
                if first_use:
                    pe.wait_ge(ring_lo, NM)
                elif bk == 6:
                    pe.wait_ge(ln_u[2], t)
                for c in range(DC):
                    b_, q = c // 2, bass.ts(c % 2, P)
                    three_pass(pe, bank[bk][:, :], x2S[:, b_, 0, q], x2S[:, b_, 1, q],
                               ringS[:, c // 2, 0, bass.ts(c % 2, D)], ringS[:, c // 2, 1, bass.ts(c % 2, D)],
                               c == 0, False)

            def turn_z(t):
                pe.wait_ge(zm_ok, t + 1)
                pe.transpose(bank[7][:, P:2 * P], zm, ident[:, :]).then_inc(zmT_ps, 1)

            def lora(t, bk=6):
                pe.wait_ge(zmT_ok, t + 1)
                pe.matmul(bank[bk][:, :], zmT[:, :], lbS[:, :], start=False, stop=True).then_inc(ffn_ps, 1)

            def tail(t, par, d=True, a=True, f=True, first_d=False, first_f=False):
                if d:
                    down(t, par, 0, first_d)
                if a:
                    turn_x1(t - 1)
                if f:
                    turn_x2(t - 2, par)
                if d:
                    down(t, par, 1, first_d)
                if a:
                    attend(t - 1, 1 - par)
                if f:
                    route(t - 2)
                    base(t - 2, first_f)
                if a:
                    turn_ex(t - 1)
                if d:
                    down(t, par, 2, first_d)
                if f:
                    turn_z(t - 2)
                if a:
                    mix(t - 1)
                if d:
                    down(t, par, 3, first_d)
                if f:
                    lora(t - 2)

            pe.wait_ge(w_lo, LOOP_CHUNK + NM // 2)
            pe.wait_ge(lb_ok, 2)
            tail(0, 0, a=False, f=False, first_d=True)
            tail(1, 1, f=False, first_d=True)
            tail(2, 0, first_f=True)
            with pe.Fori(1, B // 2 - 1) as j:
                tail(2 * j + 1, 1)
                tail(2 * j + 2, 0)
            last = B - 1
            down(last, 1, 0, False, END_SEGS)
            turn_x1(last - 1)
            turn_x2(last - 2, 1)
            down(last, 1, 1, False, END_SEGS)
            attend(last - 1, 0)
            down(last, 1, 2, False, END_SEGS)
            turn_ex(last - 1)
            down(last, 1, 3, False, END_SEGS)
            mix(last - 1)
            down(last, 1, 4, False, END_SEGS)
            route(last - 2)
            base(last - 2)
            turn_x2(last - 1, 0)
            turn_x1(last)
            turn_z(last - 2)
            attend(last, 1)
            lora(last - 2)
            turn_ex(last)
            route(last - 1)
            mix(last)
            base(last - 1)
            turn_x2(last, 1)
            keep_warm(4, 2, wdS[:, 0, 0:P], wdS[:, 0, 0:D])
            turn_z(last - 1)
            route(last, bk=1)
            lora(last - 1)
            base(last, bk=0)
            turn_z(last)
            lora(last, bk=0)

        @block.scalar
        def _(act):
            def hi_part(n, dst):
                landed = sum(raw_slot(i) == raw_slot(n) for i in range(n + 1))
                act.wait_ge(raw_in[raw_slot(n)], 16 * landed)
                act.activation(dst, raw[:, raw_slot(n), :], ACT.Copy).then_inc(w_hi, 1)

            def ring_hi(n):
                if n >= 2:
                    act.wait_ge(ip_done, 4 * (n - 1))
                hi_part(n, ringS[:, n % 2, 0, :])

            def squares(i, t, src, squared):
                act.activation(sq_out, src, ACT.Square, accum_out=ssq[:, i, t:t + 1]).then_inc(squared, 1)

            def rms(i, t0, t1, squared, logged, done):
                r = rst[:, i, t0:t1]
                act.wait_ge(squared, t1)
                act.activation(r, ssq[:, i, t0:t1], ACT.Ln, bias=epsc[:, :], scale=1.0 / D).then_inc(logged, t1 - t0)
                act.wait_ge(logged, t1)
                act.activation(r, r, ACT.Exp, scale=-0.5).then_inc(done, t1 - t0)

            def norm1(t0, t1):
                for t in range(t0, t1):
                    act.wait_ge(x_in[t], 16)
                    if t:
                        act.wait_ge(sq1, t)
                    squares(0, t, rows[:, t, :], sq1)
                if t0 == 0:
                    act.wait_ge(vec_setup, 1)
                rms(0, t0, t1, sq1, lr1, rs1)

            def hi_of_hT(t):
                act.wait_ge(hT_ps, t + 1)
                act.activation(token_cols(t, 0), blocks(bank[t % 2][:, :]), ACT.Copy).then_inc(hT_hi, 1)

            def softplus(hf):
                v = negcs[:, half(hf)]
                act.wait_ge(sp_step, 3 * (hf + 1))
                act.activation(v, v, ACT.Exp).then_inc(sp_exp, 1)
                act.wait_ge(sp_exp, hf + 1)
                act.activation(v, v, ACT.Ln, bias=onec[0:H, :]).then_inc(sp_ln, 1)

            def conv_last_tap(i):
                m, n = i // 2, conv_product(i)
                act.wait_ge(ip_done, n + 1)
                if i >= 2:
                    act.wait_ge(cv_done, i - 1)
                act.activation(acc[:, i % 2, :], bank[IN_BANK[n]][:, :], ACT.Identity,
                               bias=cb[:, m:m + 1], scale=cw[:, m, 3:4]).then_inc(cv_init, 1)

            def conv_silu(i):
                m, hf = i // 2, i % 2
                act.wait_ge(cv_tap, 3 * (i + 1))
                dst = xT[:, half(hf)] if m == 0 else bT[:, half(hf)] if m == 1 else cT[:, m - 2, half(hf)]
                act.activation(dst, acc[:, i % 2, :], ACT.Silu).then_inc(cv_done, 1)

            def z_silu(i):
                n = N_DVE_IP + i
                act.wait_ge(ip_done, n + 1)
                if i == 0:
                    act.wait_ge(lb_ok, 2)
                act.activation(szT[:, i // 2, half(i % 2)], bank[IN_BANK[n]][:, :], ACT.Silu).then_inc(z_done, 1)

            def decay(b):
                act.wait_ge(s1_done, b + 1)
                if b >= 2:
                    act.wait_ge(y_ps, b - 1)
                act.activation(xb[:, b % 2, :], bank[5][:, 0:P + 2 * H], ACT.Copy).then_inc(xb_ok, 1)
                act.wait_ge(xb_ok, b + 1)
                for h in range(H):
                    act.activation(dec[:, b % 2, h, :], bank[b % 2][:, bass.ts(h, L)], ACT.Exp,
                                   bias=xb[:, b % 2, P + h:P + h + 1], scale=-1.0).then_inc(dec_exp, 1)

            def hi_of_y(b):
                act.wait_ge(y_gated, b + 1)
                act.activation(token_cols(b, 0), blocks(hn[:, b % 2, :]), ACT.Copy).then_inc(y_hi, 1)

            def norm2(b):
                act.wait_ge(h_ok, b + 1)
                squares(1, b, acc[:, b % 2, :], sq2)
                rms(1, b, b + 1, sq2, lr2, rs2)

            def hi_of_h2(b, bk):
                act.wait_ge(h2_ps, b + 1)
                act.activation(token_cols(b, 0), blocks(bank[bk][:, :]), ACT.Copy).then_inc(h2_hi, 1)

            act.preload_act_table_set(LN_EXP)
            norm1(0, 2)
            norm1(2, HB)
            hi_of_hT(0)
            hi_part(0, ringS[:, 0, 0, :])
            hi_of_hT(1)
            hi_of_hT(2)
            norm1(HB, HB + 2)
            hi_of_hT(3)
            norm1(HB + 2, B)
            ring_hi(1)
            for t in range(HB, B):
                hi_of_hT(t)
            conv_last_tap(0)
            act.wait_ge(const_in, 16 * N_CONST)
            act.activation(expa[:, :], alog[:, :], ACT.Exp).then_inc(expa_ok, 1)
            softplus(0)
            softplus(1)
            for i in range(1, 2 * N_CONV):
                conv_last_tap(i)
                conv_silu(i - 1)
                if i % 4 == 1:
                    ring_hi(2 + i // 4)
            conv_silu(2 * N_CONV - 1)
            for i in range(4):
                z_silu(i)
            ring_hi(IN_CHUNKS - 1)
            act.preload_act_table_set(LN_EXP)
            decay(0)
            decay(1)
            for i in range(4, 2 * H):
                z_silu(i)
                if i in (4, 5):
                    hi_part(OUT_CHUNK + i - 4, wdS[:, 0, bass.ts(i - 4, CH)])
            act.preload_act_table_set(LN_EXP)
            for b in range(B + 1):
                if b < B:
                    hi_of_y(b)
                if b >= 3:
                    hi_of_h2(b - 3, 4)
                if b + 2 < B:
                    decay(b + 2)
                if b >= 1:
                    norm2(b - 1)
                if b == 3:
                    for i in range(2):
                        act.wait_ge(ip_done, 2 * N_IN)
                        hi_part(GU_CHUNK + i, ringS[:, i, 0, :])
            hi_of_h2(B - 2, 6)
            hi_of_h2(B - 1, 7)

            def sg(v, par, hf, first_use):
                act.wait_ge(gu_done, v + 1)
                if not first_use:
                    act.wait_ge(hid_ok, v - 1)
                act.activation(hn[:, par, :], bank[4 * par + 2 * hf][:, :], ACT.Silu).then_inc(sg_ok, 1)

            landed = [sum(raw_slot(n) == i for n in range(LOOP_CHUNK)) for i in range(RAW)]

            def loop_hi(j, i, dst):
                act.wait_ge(raw_in[i], 16 * j + 16 * (landed[i] + 1))
                act.activation(dst, raw[:, i, :], ACT.Copy).then_inc(w_hi, 1)

            def pair(j, first_use, last=False):
                sg(4 * j, 0, 0, first_use)
                sg(4 * j + 1, 1, 0, first_use)
                loop_hi(j, 0, wdS_t[:, bass.ds(j * CH, CH)])
                if last:
                    act.wait_ge(hid_ok, 2 * NM - 2)
                    act.activation(hidS[:, 0, 0, :], big[:, 0:NM * P], ACT.Copy).then_inc(hid_hi, 1)
                sg(4 * j + 2, 0, 1, False)
                loop_hi(j, 1, ringS[:, 0, 0, :])
                sg(4 * j + 3, 1, 1, False)

            pair(0, True)
            loop_hi(0, 2, ringS[:, 1, 0, :])
            with act.Fori(1, NM // 2 - 1) as j:
                pair(j, False)
                loop_hi(j, 2, ringS[:, 1, 0, :])
            pair(NM // 2 - 1, False, last=True)
            loop_hi(NM // 2 - 1, 2, ringS[:, 1, 0, :])

            def split_hid(t, par, first_use=False):
                if not first_use:
                    act.wait_ge(down_ps, t - 1)
                act.activation(hidS[:, par, 0, :], big[:, bass.ds(t * (NM * P), NM * P)], ACT.Copy) \
                    .then_inc(hid_hi, 1)

            def rstd(i, t, slot=None):
                k = i if slot is None else slot
                act.wait_ge(ln_mv[i], t + 1)
                act.activation(lrs[:, k:k + 1], mv[:, k, 1:2], ACT.Ln, bias=epsc[:, :]).then_inc(ln_log[i], 1)
                act.wait_ge(ln_log[i], t + 1)
                act.activation(lrs[:, k:k + 1], lrs[:, k:k + 1], ACT.Exp, scale=-0.5).then_inc(ln_rs[i], 1)

            def store(t, u=u3):
                act.wait_ge(ln_out[2], t + 1)
                act.dma_start(out[bass.ds(t, 1)].rearrange("a p n -> (a p) n"), u).then_inc(stored, 16)

            def copy_q(t):
                act.wait_ge(q_ps, t + 1)
                act.activation(qT, bank[2][:, :], ACT.Copy).then_inc(q_ok, 1)

            def copy_x2(t):
                act.wait_ge(x2_ps, t + 1)
                act.activation(x2T, bank[3][:, :], ACT.Copy).then_inc(x2_ok, 1)

            def exp_scores(t):
                act.wait_ge(mx_ok, t + 1)
                act.activation(ex, bank[4][:, 0:P], ACT.Exp, bias=sm[:, 0:1], accum_out=sm[:, 1:2]) \
                    .then_inc(ex_ok, 1)
                act.wait_ge(exT_ps, t + 1)
                act.activation(exT, bank[4][:, P:2 * P], ACT.Copy).then_inc(exT_ok, 1)

            def copy_z(t):
                act.wait_ge(zmT_ps, t + 1)
                act.activation(zmT[:, :], bank[7][0:3 * E * RANK, P:2 * P], ACT.Copy).then_inc(zmT_ok, 1)

            def tail(t, par, a=True, f=True, g=True, split=True, first_split=False):
                if a:
                    rstd(0, t - 1)
                if g:
                    rstd(2, t - 3)
                if split:
                    split_hid(t + 1, 1 - par, first_split)
                if a:
                    copy_q(t - 1)
                if f:
                    copy_x2(t - 2)
                if g:
                    store(t - 3)
                if a:
                    exp_scores(t - 1)
                if f:
                    copy_z(t - 2)
                if a:
                    rstd(1, t - 1)

            act.preload_act_table_set(LN_EXP)
            act.wait_ge(hid_ok, 2 * NM)
            tail(0, 0, a=False, f=False, g=False, first_split=True)
            tail(1, 1, f=False, g=False)
            tail(2, 0, g=False)
            with act.Fori(1, B // 2 - 1) as j:
                tail(2 * j + 1, 1)
                tail(2 * j + 2, 0)
            last = B - 1
            rstd(0, last - 1)
            rstd(2, last - 3)
            copy_q(last - 1)
            copy_x2(last - 2)
            store(last - 3)
            exp_scores(last - 1)
            rstd(1, last - 1)
            rstd(0, last)
            copy_x2(last - 1)
            copy_q(last)
            copy_z(last - 2)
            exp_scores(last)
            rstd(1, last)
            copy_x2(last)
            copy_z(last - 1)
            rstd(2, last - 2)
            store(last - 2)
            copy_z(last)
            rstd(2, last - 1)
            rstd(2, last, slot=0)
            store(last - 1, u1)
            store(last, u_last)

        @block.vector
        def _(v):
            v.memset(epsc[:, :], EPS)
            v.memset(idle, 0.0).then_inc(idle_ok, 1)
            v.memset(ones[:, :], 1.0)
            v.memset(onec[:, :], 1.0).then_inc(vec_setup, 1)

            def norm1(t):
                v.wait_ge(rs1, t + 1)
                if t == 0:
                    v.wait_ge(ln1_in, 16)
                if t >= 2:
                    v.wait_ge(hT_ps, t - 1)
                v.scalar_tensor_tensor(out=hn[:, t % 2, :], in0=rows[:, t, :], scalar=rst[:, 0, t:t + 1],
                                       in1=ln1r, op0=ALU.mult, op1=ALU.mult).then_inc(hn1, 1)

            def low(t, src, hi_ready, done):
                v.wait_ge(hi_ready, t + 1)
                v.tensor_tensor(token_cols(t, 1), blocks(src), token_cols(t, 0).bitcast(F32),
                                ALU.subtract).then_inc(done, 1)

            def low1(t):
                low(t, bank[t % 2][:, :], hT_hi, hT_lo)

            for t0 in (0, HB):
                norm1(t0)
                for t in range(t0 + 1, t0 + HB):
                    norm1(t)
                    low1(t - 1)
                low1(t0 + HB - 1)

            def softplus_in(hf):
                n = IN_ORDER.index((0, hf))
                dst, n_ps = negcs[:, half(hf)], bank[IN_BANK[n]][0:H, :]
                v.wait_ge(ip_done, n + 1)
                if hf == 0:
                    v.wait_ge(const_in, 16 * N_CONST)
                v.tensor_scalar(dt_row[:, half(hf)], n_ps, dtb[:, 0:1], 0.0, ALU.add, ALU.max).then_inc(sp_step, 1)
                v.tensor_scalar(dst, n_ps, dtb[:, 0:1], None, ALU.add).then_inc(sp_step, 1)
                v.wait_ge(sp_step, 3 * hf + 2)
                v.scalar_tensor_tensor(out=dst, in0=dst, scalar=-1.0, in1=dst, op0=ALU.mult, op1=ALU.min) \
                    .then_inc(sp_step, 1)
                v.sem_inc(ip_used, 1)

            def time_steps(hf):
                h_ = half(hf)
                v.wait_ge(sp_ln, hf + 1)
                v.tensor_tensor(dt_row[:, h_], dt_row[:, h_], negcs[:, h_], ALU.add).then_inc(dt_ok, 1)
                v.wait_ge(dt_ok, hf + 1)
                v.wait_ge(expa_ok, 1)
                v.tensor_scalar(negcs[:, h_], dt_row[:, h_], expa[:, 0:1], None, ALU.mult).then_inc(a_ok, 1)
                v.wait_ge(a_ok, hf + 1)
                for b in range(HB * hf, HB * (hf + 1)):
                    v.tensor_tensor_scan(negcs[:, tok(b)], ones[:, :], negcs[:, tok(b)], 0.0,
                                         ALU.mult, ALU.add).then_inc(cs_ok, 1)

            def conv_taps(i):
                m = i // 2
                src = bank[IN_BANK[conv_product(i)]][:, :].rearrange("p (b q) -> p b q", b=HB)
                dst = acc[:, i % 2, :].rearrange("p (b q) -> p b q", b=HB)
                v.wait_ge(cv_init, i + 1)
                for s in range(1, 4):
                    if s > 1:
                        v.wait_ge(cv_tap, 3 * i + s - 1)
                    v.scalar_tensor_tensor(out=dst[:, :, s:L], in0=src[:, :, 0:L - s],
                                           scalar=cw[:, m, 3 - s:4 - s], in1=dst[:, :, s:L],
                                           op0=ALU.mult, op1=ALU.add).then_inc(cv_tap, 1)
                v.wait_ge(cv_tap, 3 * i + 3)
                v.sem_inc(ip_used, 1)

            softplus_in(0)
            conv_taps(0)
            softplus_in(1)
            conv_taps(1)
            for i in range(2, 2 * N_CONV):
                conv_taps(i)
            time_steps(0)
            v.wait_ge(pool_setup, 8)
            for h in range(H):
                mm = v.tensor_scalar(dI[:, h, :], ident[:, :], dsk[:, h:h + 1], None, ALU.mult)
            mm.then_inc(vec_setup, 1)
            time_steps(1)

            def att(b):
                v.wait_ge(dec_exp, H * (b + 1))
                for h in range(H):
                    v.scalar_tensor_tensor(out=dec[:, b % 2, h, :], in0=bank[6][:, bass.ts(h, L)],
                                           scalar=xb[:, b % 2, P + H + h:P + H + h + 1],
                                           in1=dec[:, b % 2, h, :], op0=ALU.mult, op1=ALU.mult).then_inc(att_ok, 1)

            def gate_y(b):
                v.wait_ge(y_ps, b + 1)
                if b == 0:
                    v.wait_ge(z_done, 2 * H)
                v.tensor_tensor(blocks(hn[:, b % 2, :]), blocks(bank[7][:, :]), szT[:, :, tok(b)], ALU.mult) \
                    .then_inc(y_gated, 1)

            def add_h(b):
                v.wait_ge(op_done, b + 1)
                if b >= 2:
                    v.wait_ge(h2_ps, b - 1)
                v.tensor_tensor(acc[:, b % 2, :], bank[2 + b % 2][:, :], rows[:, b, :], ALU.add).then_inc(h_ok, 1)

            def norm2(b):
                v.wait_ge(rs2, b + 1)
                v.wait_ge(hx_ok, b + 1)
                v.scalar_tensor_tensor(out=acc[:, b % 2, :], in0=acc[:, b % 2, :], scalar=rst[:, 1, b:b + 1],
                                       in1=ln2r, op0=ALU.mult, op1=ALU.mult).then_inc(hn2, 1)

            att(0)
            att(1)
            for b in range(B + 1):
                if b < B:
                    gate_y(b)
                    low(b, hn[:, b % 2, :], y_hi, y_lo)
                if b >= 3:
                    low(b - 3, bank[4][:, :], h2_hi, h2_lo)
                if b >= 2:
                    norm2(b - 2)
                if b + 2 < B:
                    att(b + 2)
                if b >= 1:
                    add_h(b - 1)
            norm2(B - 1)
            low(B - 2, bank[6][:, :], h2_hi, h2_lo)
            low(B - 1, bank[7][:, :], h2_hi, h2_lo)

            def hidden(n, m, par, hf):
                dst = hid[:, HB * hf:HB * (hf + 1), bass.ds(m * P, P)]
                v.wait_ge(sg_ok, n + 1)
                v.tensor_tensor(dst, blocks(hn[:, par, :]), blocks(bank[4 * par + 2 * hf + 1][:, :]), ALU.mult) \
                    .then_inc(hid_ok, 1)

            def ring_low(j, par):
                v.wait_ge(w_hi, 3 * j + (LOOP_CHUNK + par + 2))
                v.tensor_tensor(ringS[:, par, 1, :], raw[:, par + 1, :], ringS[:, par, 0, :].bitcast(F32),
                                ALU.subtract).then_inc(ring_lo, 1)

            def pair(j, last=False):
                hidden(4 * j, 2 * j, 0, 0)
                hidden(4 * j + 1, 2 * j + 1, 1, 0)
                if last:
                    v.wait_ge(hid_hi, 1)
                    v.tensor_tensor(hidS[:, 0, 1, :], big[:, 0:NM * P], hidS[:, 0, 0, :].bitcast(F32),
                                    ALU.subtract).then_inc(hid_lo, 1)
                hidden(4 * j + 2, 2 * j, 0, 1)
                ring_low(j, 0)
                hidden(4 * j + 3, 2 * j + 1, 1, 1)

            with v.Fori(0, NM // 2 - 1) as j:
                pair(j)
                ring_low(j, 1)
            pair(NM // 2 - 1, last=True)
            ring_low(NM // 2 - 1, 1)

            def split_hid(t, par):
                v.wait_ge(hid_hi, t + 1)
                v.tensor_tensor(hidS[:, par, 1, :], big[:, bass.ds(t * (NM * P), NM * P)],
                                hidS[:, par, 0, :].bitcast(F32), ALU.subtract).then_inc(hid_lo, 1)

            def moments(i, t, u, slot=None):
                k = i if slot is None else slot
                v.wait_ge(ln_u[i], t + 1)
                v.bn_stats(stats[:, k, :], u).then_inc(ln_st[i], 1)
                v.wait_ge(ln_st[i], t + 1)
                v.bn_aggr(mv[:, k, :], stats[:, k, :]).then_inc(ln_mv[i], 1)

            def normed(i, t, u, slot=None):
                k = i if slot is None else slot
                v.wait_ge(ln_rs[i], t + 1)
                v.tensor_scalar(u, u, mv[:, k, 0:1], lrs[:, k:k + 1], ALU.subtract, ALU.mult).then_inc(ln_out[i], 1)

            def route(t, bk=7):
                v.wait_ge(route_ps, t + 1)
                v.tensor_tensor(lg[:, 0, :], bank[bk][:, 0:E], eb[:, :], ALU.add).then_inc(lg_step, 1)
                v.wait_ge(lg_step, 5 * t + 1)
                v.tensor_reduce(gm[:, 0:1], lg[:, 0, :], AX.X, ALU.max).then_inc(lg_step, 1)
                v.wait_ge(lg_step, 5 * t + 2)
                v.scalar_tensor_tensor(out=lg[:, 1, :], in0=lg[:, 0, :], scalar=gm[:, 0:1], in1=codes[:, :],
                                       op0=ALU.is_equal, op1=ALU.mult).then_inc(lg_step, 1)
                v.wait_ge(lg_step, 5 * t + 3)
                v.tensor_reduce(gm[:, 1:2], lg[:, 1, :], AX.X, ALU.max).then_inc(lg_step, 1)
                v.wait_ge(lg_step, 5 * t + 4)
                v.tensor_scalar(lg[:, 2, :], lg[:, 1, :], gm[:, 1:2], None, ALU.is_equal).then_inc(lg_step, 1)
                v.wait_ge(lg_step, 5 * t + 5)
                er = E * RANK
                z = zm[:, 3 * er:4 * er]
                v.tensor_tensor(z.rearrange("p (e r) -> p e r", e=E),
                                bank[bk][:, E:E + er].rearrange("p (e r) -> p e r", e=E),
                                lg[:, 2, :].unsqueeze(2).broadcast_to([P, E, RANK]), ALU.mult).then_inc(z_step, 1)
                v.wait_ge(z_step, 2 * t + 1)
                v.tensor_copy(zm[:, 0:4 * er].rearrange("p (a b r) -> p a b r", a=2, b=2)[:, :, 0, :].bitcast(F32R),
                              z.unsqueeze(1).broadcast_to([P, 2, er])).then_inc(z_step, 1)
                v.wait_ge(z_step, 2 * t + 2)
                v.tensor_tensor(zm[:, er:2 * er].bitcast(F32R), z, zm[:, 0:er], ALU.subtract).then_inc(zm_ok, 1)

            def add_mlp(t, par):
                v.wait_ge(down_ps, t + 1)
                v.tensor_tensor(u1, bank[par][:, :], rows[:, bass.ds(t, 1), :].rearrange("p a n -> p (a n)"),
                                ALU.add).then_inc(ln_u[0], 1)

            def add_ffn(t, par, u=u3, bk=6, stored_tiles=None):
                v.wait_ge(ffn_ps, t + 1)
                if stored_tiles is not None:
                    v.wait_ge(stored, 16 * stored_tiles)
                v.tensor_tensor(u, bank[bk][:, :], u2[:, par, :], ALU.add).then_inc(ln_u[2], 1)

            def split_x2(t):
                v.wait_ge(x2_ok, t + 1)
                src = x2T.rearrange("p (b n) -> p b n", b=2)
                v.tensor_copy(x2S[:, :, 0, :], src).then_inc(x2_hi, 1)
                v.wait_ge(x2_hi, t + 1)
                v.tensor_tensor(x2S[:, :, 1, :], src, x2S[:, :, 0, :].bitcast(F32), ALU.subtract).then_inc(x2_lo, 1)

            def row_max(t):
                v.wait_ge(sc_ps, t + 1)
                v.tensor_reduce(sm[:, 0:1], bank[4][:, 0:P], AX.X, ALU.max, negate=True).then_inc(mx_ok, 1)

            def add_attention(t, par):
                v.wait_ge(ex_ok, t + 1)
                v.reciprocal(sm[:, 2:3], sm[:, 1:2]).then_inc(rinv_ok, 1)
                v.wait_ge(rinv_ok, t + 1)
                v.wait_ge(pv_ps, t + 1)
                v.scalar_tensor_tensor(out=u2[:, par, :], in0=bank[5][:, :], scalar=sm[:, 2:3], in1=u1,
                                       op0=ALU.mult, op1=ALU.add).then_inc(ln_u[1], 1)

            def tail(t, par, a=True, f=True, g=True, split=True, first_g=False):
                if a:
                    add_mlp(t - 1, 1 - par)
                    moments(0, t - 1, u1)
                if g:
                    add_ffn(t - 3, 1 - par, stored_tiles=None if first_g else t - 3)
                    moments(2, t - 3, u3)
                if a:
                    normed(0, t - 1, u1)
                if g:
                    normed(2, t - 3, u3)
                if f:
                    split_x2(t - 2)
                if a:
                    row_max(t - 1)
                if split:
                    split_hid(t + 1, 1 - par)
                if f:
                    route(t - 2)
                if a:
                    add_attention(t - 1, 1 - par)
                    moments(1, t - 1, u2[:, 1 - par, :])
                    normed(1, t - 1, u2[:, 1 - par, :])

            v.wait_ge(zm_clear, 1)
            tail(0, 0, a=False, f=False, g=False)
            tail(1, 1, f=False, g=False)
            tail(2, 0, g=False)
            tail(3, 1, first_g=True)
            tail(4, 0)
            with v.Fori(2, B // 2 - 1) as j:
                tail(2 * j + 1, 1)
                tail(2 * j + 2, 0)
            last = B - 1
            add_mlp(last - 1, 0)
            moments(0, last - 1, u1)
            add_ffn(last - 3, 0, stored_tiles=last - 3)
            moments(2, last - 3, u3)
            normed(0, last - 1, u1)
            normed(2, last - 3, u3)
            split_x2(last - 2)
            row_max(last - 1)
            add_attention(last - 1, 0)
            moments(1, last - 1, u2[:, 0, :])
            normed(1, last - 1, u2[:, 0, :])
            add_mlp(last, 1)
            moments(0, last, u1)
            normed(0, last, u1)
            route(last - 2)
            row_max(last)
            split_x2(last - 1)
            add_ffn(last - 2, 1, stored_tiles=last - 2)
            add_attention(last, 1)
            moments(1, last, u2[:, 1, :])
            normed(1, last, u2[:, 1, :])
            route(last - 1)
            moments(2, last - 2, u3)
            split_x2(last)
            normed(2, last - 2, u3)
            route(last, bk=1)
            add_ffn(last - 1, 0, u=u1)
            moments(2, last - 1, u1)
            add_ffn(last, 1, u=u_last, bk=0)
            moments(2, last, u_last, slot=0)
            normed(2, last - 1, u1)
            normed(2, last, u_last, slot=0)


def kernel(**inputs):
    import numpy as np
    from concourse import bacc
    from concourse.bass_utils import run_bass_kernel_spmd

    get = {k.replace("L0_", ""): np.asarray(v) for k, v in inputs.items()}

    def stationary(wT):
        return wT.reshape(DC, P, -1, P).transpose(2, 1, 0, 3).reshape(-1, P, D)

    w_inT = get["attn_w_in"].T
    inner = H * P
    dt_block = np.zeros((D, P), w_inT.dtype)
    dt_block[:, 0:H] = w_inT[:, 2 * inner + 2 * P:]
    in_blocks = stationary(np.concatenate([dt_block, w_inT[:, inner:2 * inner + 2 * P], w_inT[:, 0:inner],
                                           np.zeros((D, P), w_inT.dtype)], axis=1))
    gate, up = (stationary(get[k].T) for k in ("attn_gate_w", "attn_up_w"))

    def pairs(blocks):
        return blocks.reshape(-1, 2, P, D).transpose(0, 2, 1, 3).reshape(-1, P, CH)

    w_in = pairs(in_blocks)
    w_gu = np.concatenate([gate, up], axis=2)
    w_out, w_down, w_base = (pairs(get[k].T.reshape(-1, P, D)) for k in ("attn_w_out", "attn_down_w", "ffn_W_up"))
    ring = np.concatenate([w_gu, w_base])
    loop = [c for j in range(NM // 2) for c in (w_down[j], ring[2 * j + 2], ring[2 * j + 3])]
    wstream = np.concatenate([w_in, w_out, ring[0:2], np.stack(loop)])

    gate_lora = np.concatenate([get["ffn_gate_w"], get["ffn_lora_A"].reshape(E * RANK, D)]).T
    ctx = get["ctx_4096"]
    ins = {
        "x": get["x"], "ctx": ctx,
        "ctxT": ctx.transpose(0, 2, 1).reshape(B, DC, P, L).transpose(0, 2, 1, 3).reshape(B, P, D),
        "wstream": wstream,
        "conv_w": get["attn_conv_w"].reshape(N_CONV, P, 4).transpose(1, 0, 2),
        "conv_b": get["attn_conv_b"].reshape(N_CONV, P).T,
        "a_log": get["attn_A_log"].reshape(H, 1), "d_skip": get["attn_D"],
        "dt_bias": get["attn_dt_bias"].reshape(H, 1), "ln1_w": get["attn_ln1_w"], "ln2_w": get["attn_ln2_w"],
        "gate_lora": gate_lora.reshape(DC, P, -1).transpose(1, 0, 2), "expert_bias": get["ffn_expert_bias"],
        "lora_b": get["ffn_lora_B"].transpose(0, 2, 1).reshape(E * RANK, D),
    }
    nc = bacc.Bacc("TRN2", target_bir_lowering=False, num_devices=1)
    arrays, args = {}, []
    for name, a in ins.items():
        arrays[name] = np.ascontiguousarray(a)
        args.append(nc.dram_tensor(name, a.shape, F32, kind="ExternalInput").ap())
    args.append(nc.dram_tensor("out", (B, L, D), F32, kind="ExternalOutput").ap())
    build(nc, *args)
    r = run_bass_kernel_spmd(nc, [arrays], core_ids=[0])
    return r.results[0]["out"]
```
